# Optimizing a Trainium2 kernel written in Bass

```python
import numpy as np
import jax
import jax.numpy as jnp

def _softmax(x, axis=-1):
    return jax.nn.softmax(x, axis=axis)

def _gelu(x):
    return jax.nn.gelu(x, approximate=True)

def _silu(x):
    return jax.nn.silu(x)

def _sigmoid(x):
    return jax.nn.sigmoid(x)

def _layernorm(x, axis=-1, eps=1e-05):
    m = jnp.mean(x, axis=axis, keepdims=True)
    v = jnp.var(x, axis=axis, keepdims=True)
    return (x - m) / jnp.sqrt(v + eps)

def _scatter_add(tgt, idx, src, axis=0):
    return tgt.at[idx].add(src)

def _segment_sum(src, seg, n):
    return jax.ops.segment_sum(src, seg, n)
kernel_name = 'mk_decoder_preln_d1_seqx_r4_76d905'

def setup_inputs(seed: int=0):
    np.random.seed(seed)
    _w = jnp.asarray

    def _rec_inputs():
        import jax
        import jax.numpy as jnp
        _rk = jax.random.key(seed)
        x = -7.109e-05 + 0.9999 * jax.random.normal(jax.random.fold_in(_rk, 1), (8, 112, 1024), jnp.float32)
        _lenS = 112 - jax.random.randint(jax.random.fold_in(_rk, 7), (8,), 0, max(1, 112 // 4) + 1, jnp.int32)
        _lenS2 = 375 - jax.random.randint(jax.random.fold_in(_rk, 8), (8,), 0, max(1, 375 // 4) + 1, jnp.int32)
        _ctx_4096P = jax.random.normal(jax.random.fold_in(_rk, 11), (8, 16, 1024), jnp.float32)
        _ctx_4096c = jax.random.dirichlet(jax.random.fold_in(_rk, 511), 0.3 * jnp.ones((16,), jnp.float32), (8, 375))
        _ctx_4096t = jnp.einsum('bsk,bkd->bsd', _ctx_4096c, _ctx_4096P)
        _ctx_4096t = _ctx_4096t * jax.lax.rsqrt(jnp.mean(jnp.square(_ctx_4096t)) + 1e-12) * 0.953939
        ctx_4096 = -0.00010331 + 0.999899 * (_ctx_4096t + 0.3 * jax.random.normal(jax.random.fold_in(_rk, 611), (8, 375, 1024), jnp.float32))
        return (x, ctx_4096)
    x, ctx_4096 = _rec_inputs()

    def _L0_attn_setup():
        import jax, jax.numpy as jnp
        import numpy as np
        H_M, P_M, G_M, N_M, K_CONV, CHUNK = (128, 64, 8, 128, 4, 128)
        D_MODEL = 1024
        D_INNER = H_M * P_M
        CONV_DIM = D_INNER + 2 * G_M * N_M
        PROJ_DIM = D_INNER + CONV_DIM + H_M
        EPS = 1e-05

        def segsum(x):
            l = x.shape[-1]
            xe = jnp.broadcast_to(x[..., None], x.shape + (l,))
            m1 = jnp.tril(jnp.ones((l, l), dtype=bool), -1)
            s = jnp.cumsum(jnp.where(m1, xe, 0.0), axis=-2)
            m2 = jnp.tril(jnp.ones((l, l), dtype=bool), 0)
            return jnp.where(m2, s, -jnp.inf)

        def causal_conv(x, w, bconv):
            k = w.shape[1]
            s = x.shape[1]
            xp = jnp.pad(x, ((0, 0), (k - 1, 0), (0, 0)))
            y = sum((xp[:, i:i + s, :] * w[:, i] for i in range(k)))
            return y + bconv
        key = jax.random.key(seed)
        ks = jax.random.split(key, 8)
        B_, S = (1, 512)
        sc = 0.02
        return {'x': jax.random.normal(ks[0], (B_, S, D_MODEL), dtype=jnp.float32), 'norm_w': jnp.ones((D_MODEL,), dtype=jnp.float32), 'in_proj_w': jax.random.normal(ks[1], (PROJ_DIM, D_MODEL), dtype=jnp.float32) * sc, 'conv_w': jax.random.normal(ks[2], (CONV_DIM, K_CONV), dtype=jnp.float32) * 0.2, 'conv_b': jnp.zeros((CONV_DIM,), dtype=jnp.float32), 'dt_bias': jax.random.uniform(ks[3], (H_M,), dtype=jnp.float32) * 0.1, 'A_log': jnp.log(1.0 + 15.0 * jax.random.uniform(ks[4], (H_M,), dtype=jnp.float32)), 'Dp': jnp.ones((H_M,), dtype=jnp.float32), 'gnorm_w': jnp.ones((D_INNER,), dtype=jnp.float32), 'out_proj_w': jax.random.normal(ks[5], (D_MODEL, D_INNER), dtype=jnp.float32) * sc}
    _L0_attn_all = _L0_attn_setup()
    _L0_attn_in = {k: v for k, v in _L0_attn_all.items() if k in ('norm_w', 'in_proj_w', 'conv_w', 'conv_b', 'dt_bias', 'A_log', 'Dp', 'gnorm_w', 'out_proj_w')}
    del _L0_attn_all

    def _L0_xattn_setup():
        import jax, jax.numpy as jnp
        import numpy as np
        key = jax.random.key(seed)
        k1, k2 = jax.random.split(key)
        B, Lq, Lk, D = (16, 256, 512, 1024)
        query = jax.random.normal(k1, (B, Lq, D), dtype=jnp.float32)
        key_t = jax.random.normal(k2, (B, Lk, D), dtype=jnp.float32)
        return {'query': query, 'key': key_t}
    _L0_xattn_all = _L0_xattn_setup()
    _L0_xattn_in = {k: v for k, v in _L0_xattn_all.items() if k in ()}
    del _L0_xattn_all

    def _L0_ffn_setup():
        import jax, jax.numpy as jnp
        import numpy as np

        @jax.custom_vjp
        def ste_sign(w):
            return jnp.sign(w)

        def _ste_fwd(w):
            return (jnp.sign(w), w)

        def _ste_bwd(w, g):
            mask = ((w > -1) & (w < 1)).astype(g.dtype)
            return (g * mask,)
        ste_sign.defvjp(_ste_fwd, _ste_bwd)
        key = jax.random.key(seed)
        k = jax.random.split(key, 6)
        B, S, H, O, E = (4, 512, 1024, 1024, 8)
        return {'x': jax.random.normal(k[0], (B, S, H), dtype=jnp.float32), 'weight': jax.random.normal(k[1], (O, H), dtype=jnp.float32) * 0.02, 'bias': jax.random.normal(k[2], (O,), dtype=jnp.float32) * 0.02, 'gate_w': jax.random.normal(k[3], (E, H), dtype=jnp.float32) * 0.02, 'in_channel_scale': jax.random.normal(k[4], (E, H), dtype=jnp.float32), 'out_channel_scale': jax.random.normal(k[5], (E, O), dtype=jnp.float32)}
    _L0_ffn_all = _L0_ffn_setup()
    _L0_ffn_in = {k: v for k, v in _L0_ffn_all.items() if k in ('weight', 'bias', 'gate_w', 'in_channel_scale', 'out_channel_scale')}
    del _L0_ffn_all
    return {'x': x, 'ctx_4096': ctx_4096, 'L0_attn_norm_w': _L0_attn_in['norm_w'], 'L0_attn_in_proj_w': _L0_attn_in['in_proj_w'], 'L0_attn_conv_w': _L0_attn_in['conv_w'], 'L0_attn_conv_b': _L0_attn_in['conv_b'], 'L0_attn_dt_bias': _L0_attn_in['dt_bias'], 'L0_attn_A_log': _L0_attn_in['A_log'], 'L0_attn_Dp': _L0_attn_in['Dp'], 'L0_attn_gnorm_w': _L0_attn_in['gnorm_w'], 'L0_attn_out_proj_w': _L0_attn_in['out_proj_w'], 'L0_ffn_weight': _L0_ffn_in['weight'], 'L0_ffn_bias': _L0_ffn_in['bias'], 'L0_ffn_gate_w': _L0_ffn_in['gate_w'], 'L0_ffn_in_channel_scale': _L0_ffn_in['in_channel_scale'], 'L0_ffn_out_channel_scale': _L0_ffn_in['out_channel_scale']}

def reference(x, ctx_4096, L0_attn_norm_w, L0_attn_in_proj_w, L0_attn_conv_w, L0_attn_conv_b, L0_attn_dt_bias, L0_attn_A_log, L0_attn_Dp, L0_attn_gnorm_w, L0_attn_out_proj_w, L0_ffn_weight, L0_ffn_bias, L0_ffn_gate_w, L0_ffn_in_channel_scale, L0_ffn_out_channel_scale):
    import jax
    import jax.numpy as jnp

    def _L0_attn_ref(x, norm_w, in_proj_w, conv_w, conv_b, dt_bias, A_log, Dp, gnorm_w, out_proj_w):
        import jax, jax.numpy as jnp
        import numpy as np
        H_M, P_M, G_M, N_M, K_CONV, CHUNK = (128, 64, 8, 128, 4, 128)
        D_MODEL = 1024
        D_INNER = H_M * P_M
        CONV_DIM = D_INNER + 2 * G_M * N_M
        PROJ_DIM = D_INNER + CONV_DIM + H_M
        EPS = 1e-05

        def segsum(x):
            l = x.shape[-1]
            xe = jnp.broadcast_to(x[..., None], x.shape + (l,))
            m1 = jnp.tril(jnp.ones((l, l), dtype=bool), -1)
            s = jnp.cumsum(jnp.where(m1, xe, 0.0), axis=-2)
            m2 = jnp.tril(jnp.ones((l, l), dtype=bool), 0)
            return jnp.where(m2, s, -jnp.inf)

        def causal_conv(x, w, bconv):
            k = w.shape[1]
            s = x.shape[1]
            xp = jnp.pad(x, ((0, 0), (k - 1, 0), (0, 0)))
            y = sum((xp[:, i:i + s, :] * w[:, i] for i in range(k)))
            return y + bconv
        b, s, _ = x.shape
        residual = x
        h = x * jax.lax.rsqrt(jnp.mean(x * x, axis=-1, keepdims=True) + EPS) * norm_w
        proj = jnp.einsum('bsd,od->bso', h, in_proj_w)
        gate = proj[..., :D_INNER]
        hBC = proj[..., D_INNER:D_INNER + CONV_DIM]
        dt = proj[..., D_INNER + CONV_DIM:]
        hBC = jax.nn.silu(causal_conv(hBC, conv_w, conv_b))
        hid = hBC[..., :D_INNER].reshape(b, s, H_M, P_M)
        B = hBC[..., D_INNER:D_INNER + G_M * N_M].reshape(b, s, G_M, N_M)
        C = hBC[..., D_INNER + G_M * N_M:].reshape(b, s, G_M, N_M)
        dt = jax.nn.softplus(dt + dt_bias)
        A = -jnp.exp(A_log)
        pad = -s % CHUNK
        D_res = Dp[None, None, :, None] * hid
        hid_dt = hid * dt[..., None]
        A_full = A[None, None, :] * dt

        def padseq(t):
            return jnp.pad(t, [(0, 0), (0, pad)] + [(0, 0)] * (t.ndim - 2))
        hid_dt, A_full, Bp, Cp = (padseq(hid_dt), padseq(A_full), padseq(B), padseq(C))
        S = s + pad
        c, l = (S // CHUNK, CHUNK)
        hc = hid_dt.reshape(b, c, l, H_M, P_M)
        Ac = A_full.reshape(b, c, l, H_M).transpose(0, 3, 1, 2)
        rep = H_M // G_M
        Bh = jnp.repeat(Bp.reshape(b, c, l, G_M, N_M), rep, axis=3)
        Ch = jnp.repeat(Cp.reshape(b, c, l, G_M, N_M), rep, axis=3)
        A_cs = jnp.cumsum(Ac, axis=-1)
        L = jnp.exp(segsum(Ac))
        M = jnp.einsum('bcihn,bcjhn->bcijh', Ch, Bh) * jnp.transpose(L, (0, 2, 3, 4, 1))
        Y_diag = jnp.einsum('bcijh,bcjhp->bcihp', M, hc)
        decay_states = jnp.exp(A_cs[..., -1:] - A_cs)
        states = jnp.einsum('bclhn,bhcl,bclhp->bchpn', Bh, decay_states, hc)
        A_last = jnp.pad(A_cs[..., -1], ((0, 0), (0, 0), (1, 0)))
        decay_chunk = jnp.exp(segsum(A_last))
        states_cat = jnp.concatenate([jnp.zeros_like(states[:, :1]), states], axis=1)
        prev_states = jnp.einsum('bhij,bjhpn->bihpn', decay_chunk, states_cat)[:, :-1]
        Y_off = jnp.einsum('bclhn,bchpn,bhcl->bclhp', Ch, prev_states, jnp.exp(A_cs))
        y = (Y_diag + Y_off).reshape(b, S, H_M, P_M)[:, :s] + D_res
        y = y.reshape(b, s, D_INNER)
        yg = y * jax.nn.silu(gate)
        gsz = D_INNER // G_M
        ygr = yg.reshape(b, s, G_M, gsz)
        ygr = ygr * jax.lax.rsqrt(jnp.mean(ygr * ygr, axis=-1, keepdims=True) + EPS)
        y = ygr.reshape(b, s, D_INNER) * gnorm_w
        out = jnp.einsum('bsd,od->bso', y, out_proj_w)
        return residual + out

    def _L0_xattn_ref(query, key):
        import jax, jax.numpy as jnp
        import numpy as np
        a = jnp.einsum('bqd,bkd->bqk', query, key)
        e = jax.nn.softmax(a, axis=-1)
        c = jnp.einsum('bqk,bkd->bqd', e, key)
        return c

    def _L0_ffn_ref(x, weight, bias, gate_w, in_channel_scale, out_channel_scale):
        import jax, jax.numpy as jnp
        import numpy as np

        @jax.custom_vjp
        def ste_sign(w):
            return jnp.sign(w)

        def _ste_fwd(w):
            return (jnp.sign(w), w)

        def _ste_bwd(w, g):
            mask = ((w > -1) & (w < 1)).astype(g.dtype)
            return (g * mask,)
        ste_sign.defvjp(_ste_fwd, _ste_bwd)
        B, S, H = x.shape
        xf = x.reshape(-1, H)
        router_logits = xf @ gate_w.T
        routing = jax.nn.softmax(router_logits.astype(jnp.float32), axis=1).astype(x.dtype)
        in_scale = routing @ in_channel_scale
        out_scale = routing @ out_channel_scale
        wb = ste_sign(weight)
        out = xf * in_scale @ wb.T * out_scale + bias
        return out.reshape(B, S, -1)
    x = x + _L0_attn_ref(_layernorm(x, axis=-1), L0_attn_norm_w, L0_attn_in_proj_w, L0_attn_conv_w, L0_attn_conv_b, L0_attn_dt_bias, L0_attn_A_log, L0_attn_Dp, L0_attn_gnorm_w, L0_attn_out_proj_w)
    x = x + _L0_xattn_ref(_layernorm(x, axis=-1), ctx_4096)
    x = x + _L0_ffn_ref(_layernorm(x, axis=-1), L0_ffn_weight, L0_ffn_bias, L0_ffn_gate_w, L0_ffn_in_channel_scale, L0_ffn_out_channel_scale)
    return x

_drawn_inputs = setup_inputs


def setup_inputs(seed=0):
    import zlib

    import numpy as np

    out = dict(_drawn_inputs(seed))
    spreads = {'L0_attn_norm_w': (1.0, 0.2),
     'L0_attn_conv_b': (0.0, 0.1),
     'L0_attn_Dp': (1.0, 0.2),
     'L0_attn_gnorm_w': (1.0, 0.2)}
    factors = {'L0_attn_dt_bias': 8.0, 'L0_ffn_bias': 8.0}
    for name, (base, spread) in spreads.items():
        noise = np.random.default_rng([zlib.crc32(name.encode()), seed]).standard_normal(out[name].shape)
        drawn = base * np.exp(spread * noise) if base else spread * noise
        out[name] = jnp.asarray(drawn.astype(out[name].dtype))
    for name, factor in factors.items():
        out[name] = (out[name] * factor).astype(out[name].dtype)
    return out
```

```python
from contextlib import ExitStack

import numpy as np

import concourse.bass as bass
from concourse import mybir

F32 = mybir.dt.float32
BF16 = mybir.dt.bfloat16
ALU = mybir.AluOpType
ACT = mybir.ActivationFunctionType
AX = mybir.AxisListType

P = 128
NB, S, D = 8, 112, 1024
T = NB * S
TH = T // 2
HB = NB // 2
KD = D // P
HEADS, HP, G = 128, 64, 8
DI = HEADS * HP
KG = DI // G // P
TPG = 2 + 2 * KG + KD
RING = TPG // 2
CONV = 4
CST = 1 + 2 * (CONV - 1)
CPG = 2 + KG
NPAR = CONV + 3
EPS = 1e-5
LK, CK = 375, 3
LC = LK // CK
NE = 8
MASKED = -1e30
SEGK = 9


def bc(ap, shape):
    return ap.broadcast_to(shape)


def build(nc, x_t, w_dt, w_main, par_d, norm_w, head_par, const32, mask_d, seg_r0, seg_l0, ctx_t, ctx_n,
          w_ffn, gate_w, in_scale, out_scale, ffn_bias, out):
    with ExitStack() as ctx:
        def sb(name, shape, dt=F32, scope=ctx):
            return scope.enter_context(nc.sbuf_tensor(name, shape, dt))

        def sem(name):
            return ctx.enter_context(nc.semaphore(name))

        pA = ctx.enter_context(nc.psum_tensor("pA", [P, 2, 512], F32))
        pB = ctx.enter_context(nc.psum_tensor("pB", [P, 2, 512], F32))
        pY = ctx.enter_context(nc.psum_tensor("pY", [P, 2, 512], F32))
        pT = ctx.enter_context(nc.psum_tensor("pT", [P, 512], F32))
        pS = ctx.enter_context(nc.psum_tensor("pS", [P, 512], F32))
        pAB = [pA, pB]

        def halves(ps):
            return ps[:, :, 0:TH]

        def batches(ps):
            return ps[:, :, 0:TH].rearrange("p s (b i) -> p s b i", b=HB)

        acc = sb("acc", [P, KD, T])
        h = sb("h", [P, KD, T])
        y = sb("y", [P, KG, T])
        ring = sb("ring", [P, RING, KD, P])
        ident = sb("ident", [P, P])
        ones = sb("ones", [P, P])

        mixer = ExitStack()
        par = sb("par", [P, G * CPG, NPAR], scope=mixer)
        nw = sb("nw", [P, KD], scope=mixer)
        hpar = sb("hpar", [P, 2], scope=mixer)
        hexp = sb("hexp", [P, 1], scope=mixer)
        tri = sb("tri", [S, S], scope=mixer)
        mask = sb("mask", [S, 5, S], BF16, scope=mixer)
        seg_r = [sb(f"seg_r{i}", [SEGK, NB, 2, S], BF16, scope=mixer) for i in range(2)]
        seg_l = [sb(f"seg_l{i}", [SEGK, NB, S], BF16, scope=mixer) for i in range(2)]
        dt_t = sb("dt_t", [S, NB, HEADS], scope=mixer)
        hid = [sb(f"hid{i}", [P, T], scope=mixer) for i in range(2)]
        gate = [sb(f"gate{i}", [P, T], scope=mixer) for i in range(2)]
        th = sb("th", [P, T], scope=mixer)
        hc = sb("hc", [S, NB, P], scope=mixer)
        m_t = [sb(f"m_t{i}", [S, NB, 2, S], scope=mixer) for i in range(2)]
        g_t = sb("g_t", [S, NB, S], scope=mixer)
        sq = sb("sq", [P, T], scope=mixer)
        wdt = sb("wdt", [P, KD, P], scope=mixer)
        ssum = wdt[:].rearrange("p k c -> p (k c)")[:, 0:T]
        rs = sb("rs", [P, T], scope=mixer)
        tmp = [sq, th]
        small = sb("small", [S, NB], scope=mixer)
        diag = gate[0]
        cB, cC = hid[1], rs
        mixer.close()

        tail = ExitStack()
        wff = sb("wff", [P, KD, D], scope=tail)
        prob = [sb(f"prob{i}", [S, LK], scope=tail) for i in range(2)]
        prob_t = [sb(f"prob_t{i}", [LC, CK, S], scope=tail) for i in range(2)]
        stat = sb("stat", [S, 4, NB], scope=tail)
        ln_r = sb("ln_r", [P, T], scope=tail)
        gw = sb("gw", [P, KD, NE], scope=tail)
        isc = sb("isc", [NE, D], scope=tail)
        osc = sb("osc", [NE, D], scope=tail)
        fb = sb("fb", [P, KD], scope=tail)
        route = sb("route", [S, NB, NE], scope=tail)
        route_t = sb("route_t", [NE, T], scope=tail)
        rstat = sb("rstat", [S, 2, NB], scope=tail)
        oscale = [sb(f"oscale{i}", [P, T], scope=tail) for i in range(2)]
        tail.close()
        ctxt_sb = [ring[:].rearrange("p a b c -> p (a b c)")[:, i * 6144:i * 6144 + KD * LK]
                   .rearrange("p (k n) -> p k n", k=KD) for i in range(2)]
        ctxn_sb = [ring[:].rearrange("p a b c -> p (a b c)")[0:LC, i * 6144 + 3072:i * 6144 + 3072 + CK * D]
                   .rearrange("p (k n) -> p k n", k=CK) for i in range(2)]

        cs_pos = nc.dram_tensor("cs_pos", (HEADS, 3, T), BF16).ap()
        cs_neg = nc.dram_tensor("cs_neg", (HEADS, 3, T), BF16).ap()

        x_in = sem("x_in")
        const_in = sem("const_in")
        w_in = [sem(f"w_in{i}") for i in range(RING)]
        wdt_in = sem("wdt_in")
        seg_in = [sem(f"seg_in{i}") for i in range(2)]
        cs_out = sem("cs_out")
        ln_sum, ln_centre, ln_sq, ln_var, ln_std, ln_out, ln_own = (
            sem(x) for x in ("ln_sum", "ln_centre", "ln_sq", "ln_var", "ln_std", "ln_out", "ln_own"))
        ones_set = sem("ones_set")
        ln_tmp, acc_ln = sem("ln_tmp"), sem("acc_ln")
        dt_mm, dt_abs, dt_max, dt_act, dt_own, dt_tr, dt_copy, cs_mm, cs_split, cs_negd = (
            sem(x) for x in ("dt_mm", "dt_abs", "dt_max", "dt_act", "dt_own", "dt_tr", "dt_copy", "cs_mm", "cs_split", "cs_negd"))
        halved = sem("halved")
        proj_done = sem("proj_done")
        conv_done = sem("conv_done")
        tanh_c, silu_done = sem("tanh_c"), sem("silu_done")
        tanh_g, gated = sem("tanh_g"), sem("gated")
        seg_mm, exp_done = sem("seg_mm"), sem("exp_done")
        cb_mm, cb_copy = sem("cb_mm"), sem("cb_copy")
        tr_done, hc_done = sem("tr_done"), sem("hc_done")
        m_done = sem("m_done")
        y_mm, skip_done, yg_done, y_done, sq_done, sum_done = (
            sem(x) for x in ("y_mm", "skip_done", "yg_done", "y_done", "sq_done", "sum_done"))
        gn_mm, gn_var, gn_std, gn_r, gn_diag, gn_bc, gn_rs = (
            sem(x) for x in ("gn_mm", "gn_var", "gn_std", "gn_r", "gn_diag", "gn_bc", "gn_rs"))
        out_scaled, out_added = sem("out_scaled"), sem("out_added")
        ctx_in = [sem(f"ctx_in{i}") for i in range(2)]
        ffn_in = sem("ffn_in")
        sc_mm, mx_done, ex_done, ri_done, pn_done, pt_mm, pt_copy, xo_mm, x2_done, sub_done = (
            sem(x) for x in ("sc_mm", "mx_done", "ex_done", "ri_done", "pn_done", "pt_mm", "pt_copy", "xo_mm", "x2_done", "sub_done"))
        sign_done = sem("sign_done")
        r_mm, r_own, r_exp, r_tr, r_copy = (sem(x) for x in ("r_mm", "r_own", "r_exp", "r_tr", "r_copy"))
        is_mm, xs_done, f_mm, os_mm, os_copy, f_scaled, f_done, stored = (
            sem(x) for x in ("is_mm", "xs_done", "f_mm", "os_mm", "os_copy", "f_scaled", "f_done", "stored"))

        LAST = G - 1
        ALL_OUT = G * KD

        block = ctx.enter_context(nc.Block())

        def da_t(b):
            return m_t[0][:].rearrange("p b h i -> p (b h i)")[:, b * HEADS:(b + 1) * HEADS]

        def cs_parts(i):
            return y[:].rearrange("p k t -> p (k t)").bitcast(BF16)[:, i * 3 * T:(i + 1) * 3 * T]

        def flat(buf):
            return buf[:].rearrange("p (s n) -> p s n", s=2)

        def shifted(buf, n):
            return buf[:].rearrange("p (s b i) -> p s b i", s=2, b=HB)[:, :, :, n:S]

        @block.sync
        def _(sp):
            for i in range(2):
                k = slice(i * KD // 2, (i + 1) * KD // 2)
                sp.dma_start(acc[:, k, :], x_t.rearrange("(k p) t -> p k t", p=P)[:, k, :]).then_inc(x_in, 16)
            sp.dma_start(ident[:], const32[:, 0:P]).then_inc(const_in, 16)
            sp.dma_start(tri[:], const32[0:S, P:P + S]).then_inc(const_in, 16)
            sp.dma_start(nw[:], norm_w).then_inc(const_in, 16)
            sp.dma_start(hpar[:], head_par).then_inc(const_in, 16)
            sp.dma_start(par[:], par_d).then_inc(const_in, 16)
            sp.dma_start(mask[:], mask_d).then_inc(const_in, 16)
            sp.dma_start(wdt[:], w_dt).then_inc(wdt_in, 16)

            def load_w(tile, slot):
                sp.dma_start(ring[:, slot], w_main[bass.ds(tile, 1)].squeeze(0) if not isinstance(tile, int)
                             else w_main[tile]).then_inc(w_in[slot], 16)

            def load_seg(step, buf):
                src = cs_pos[bass.ds(step * 2, 2)].rearrange("h c (b i) -> c b h i", b=NB)
                for hh in range(2):
                    sp.dma_start(seg_r[buf][0:3, :, hh, :], src[:, :, hh, :]).then_inc(seg_in[buf], 16)
                sp.dma_start(seg_l[buf][3:SEGK], cs_neg[bass.ds(step * 2, 2)].rearrange("h c (b i) -> (h c) b i", b=NB))\
                    .then_inc(seg_in[buf], 16)

            for t in range(RING):
                load_w(t, t)
            for i in range(2):
                sp.dma_start(seg_r[i][:], seg_r0).then_inc(const_in, 16)
            for i in range(2):
                sp.dma_start(seg_l[i][:], seg_l0).then_inc(const_in, 16)
            sp.wait_ge(cs_split, 3)
            sp.dma_start(cs_pos.rearrange("h c t -> h (c t)"), cs_parts(0)).then_inc(cs_out, 16)
            sp.wait_ge(cs_negd, 1)
            sp.dma_start(cs_neg.rearrange("h c t -> h (c t)"), cs_parts(1)).then_inc(cs_out, 16)
            sp.wait_ge(cs_out, 32)
            sp.wait_ge(const_in, 16 * (6 + 4))
            for i in range(2):
                load_seg(i, i)

            def group_loads(g, tiles, segs):
                for t in range(tiles):
                    sp.wait_ge(proj_done, g * TPG + (t + 1))
                    load_w(g * TPG + (t + RING), t % RING)
                    q = (t - 2) // 2
                    if t >= 2 and t % 2 == 0 and q < segs:
                        load_seg(g * KG + (q + 2), q % 2)

            with sp.Fori(0, LAST) as g:
                group_loads(g, TPG, KG)
            for t in range(2 + 2 * (KG - 2)):
                sp.wait_ge(proj_done, LAST * TPG + t + 1)
                if t + RING < TPG:
                    load_w(LAST * TPG + t + RING, t % RING)
                q = (t - 2) // 2
                if t >= 2 and t % 2 == 0 and q < KG - 2:
                    load_seg(LAST * KG + q + 2, q % 2)

            sp.wait_ge(proj_done, G * TPG)
            for b in range(NB):
                if b >= 2:
                    sp.wait_ge(xo_mm, b - 1)
                sp.dma_start(ctxt_sb[b % 2], ctx_t[b].rearrange("(k p) n -> p k n", p=P)).then_inc(ctx_in[b % 2], 16)
                sp.dma_start(ctxn_sb[b % 2], ctx_n[b].rearrange("(k p) n -> p k n", p=LC)).then_inc(ctx_in[b % 2], 16)
                if b == 1:
                    sp.wait_ge(out_added, ALL_OUT + KD)
                    sp.dma_start(gw[:], gate_w.rearrange("(k p) e -> p k e", p=P)).then_inc(ffn_in, 16)
                    sp.dma_start(isc[:], in_scale).then_inc(ffn_in, 16)
                    sp.dma_start(osc[:], out_scale).then_inc(ffn_in, 16)
                    sp.dma_start(fb[:], ffn_bias).then_inc(ffn_in, 16)
                    sp.dma_start(wff[:], w_ffn).then_inc(ffn_in, 16)
            for o in range(KD):
                sp.wait_ge(f_done, 2 * o + 2)
                sp.dma_start(out[o * P:(o + 1) * P, :], acc[:, o, :]).then_inc(stored, 16)
            sp.wait_ge(stored, 16 * KD)

        @block.tensor
        def _(pe):
            def total(ps, src, done, value_sem=None, value=0):
                for s in range(2):
                    for k in range(KD):
                        if s == 0 and value_sem is not None:
                            pe.wait_ge(value_sem, value + k)
                        mm = pe.matmul(ps[:, s, 0:TH], ones[:], src[:, k, s * TH:(s + 1) * TH],
                                       start=(k == 0), stop=(k == KD - 1))
                mm.then_inc(done, 1)

            pe.wait_ge(x_in, 32)
            pe.wait_ge(ones_set, 1)
            total(pY, acc, ln_sum)
            total(pA, y, ln_sum, ln_sq, 1)

            pe.wait_ge(wdt_in, 16)
            for s in range(2):
                for k in range(KD):
                    if s == 0:
                        pe.wait_ge(ln_out, k + 1)
                    mm = pe.matmul(pB[:, s, 0:TH], wdt[:, k, :], h[:, k, s * TH:(s + 1) * TH],
                                   start=(k == 0), stop=(k == KD - 1))
            mm.then_inc(dt_mm, 1)
            pe.wait_ge(const_in, 16 * 10)
            for n in range(4):
                pe.wait_ge(dt_own, 2 + n // 2)
                if n == 0:
                    pe.wait_ge(ln_out, KD)
                if n >= 2:
                    pe.wait_ge(dt_copy, n - 1)
                src = [gate[0], gate[1]][n // 2]
                for b in range(HB):
                    t0 = (n % 2 * HB + b) * S
                    mm = pe.transpose([pT, pS][n % 2][0:S, b * P:(b + 1) * P], src[:, t0:t0 + S], ident[:])
                mm.then_inc(dt_tr, 1)
            pe.wait_ge(dt_copy, 4)
            for b in range(NB):
                mm = pe.matmul(pY[:, b // HB, (b % HB) * S:(b % HB + 1) * S], da_t(b), tri[:],
                               start=True, stop=True)
            mm.then_inc(cs_mm, 1)

            def project(g, t, rhs, ks, fillers=None, first=True, last=True, gate_k=None):
                ps = pAB[t % 2]
                if first:
                    pe.wait_ge(w_in[t % RING], g * 32 + 16 * (t // RING + 1))
                    free_bank(g, t)
                for k in ks:
                    if gate_k is not None:
                        gate_k(k)
                    for s in range(2):
                        mm = pe.matmul(ps[:, s, 0:TH], ring[:, t % RING, k, :], rhs[:, k, s * TH:(s + 1) * TH],
                                       start=(k == 0), stop=(k == KD - 1))
                    if k == KD - 1 and last:
                        mm.then_inc(proj_done, 1)
                    for f in (fillers or {}).get(k, []):
                        f()

            def free_bank(g, t):
                u = t - 2
                if u < 0:
                    pe.wait_ge(out_scaled, g * KD + (KD + u + 1))
                elif u < 2:
                    pe.wait_ge(conv_done, g * (CST * CPG) + CST * (u + 1))
                elif u < 2 + 2 * KG and u % 2 == 0:
                    pe.wait_ge(conv_done, g * (CST * CPG) + CST * (2 + (u - 2) // 2 + 1))
                elif u < 2 + 2 * KG:
                    pe.wait_ge(gated, g * KG + ((u - 2) // 2 + 1))
                else:
                    pe.wait_ge(out_scaled, g * KD + (KD + u - (2 + 2 * KG) + 1))

            def seg(g, q, n):
                if n == 0:
                    pe.wait_ge(seg_in[q % 2], g * (48 * KG // 2) + 48 * (q // 2 + 1))
                pe.wait_ge(exp_done, g * (4 * KG) + (4 * q + n + 1))
                pe.matmul(pS[0:S, 0:4 * S], mask[:, 4, :], mask[:, 0:4, :], start=True, stop=False,
                          skip_group_check=True)
                for j in range(2):
                    b = 2 * n + j
                    mm = pe.matmul(pS[0:S, 2 * j * S:2 * (j + 1) * S], seg_l[q % 2][:, b, :], seg_r[q % 2][:, b, :, :],
                                   start=False, stop=(j == 1), skip_group_check=True)
                mm.then_inc(seg_mm, 1)

            def turn(g, q, s):
                if s == 0:
                    pe.wait_ge(silu_done, g * CPG + (q + 3))
                    if q == 0:
                        pe.wait_ge(cb_copy, g * 2 + 2)
                    else:
                        pe.wait_ge(hc_done, g * (2 * KG) + (2 * q + 1))
                else:
                    pe.wait_ge(hc_done, g * (2 * KG) + (2 * q + 2))
                for b in range(HB):
                    t0 = (s * HB + b) * S
                    mm = pe.transpose(pT[0:S, b * P:(b + 1) * P], hid[q % 2][:, t0:t0 + S], ident[:])
                mm.then_inc(tr_done, 1)

            def cb(g, s):
                pe.wait_ge(silu_done, g * CPG + 2)
                if s == 0:
                    pe.wait_ge(hc_done, g * (2 * KG) + 1)
                else:
                    pe.wait_ge(cb_copy, g * 2 + 1)
                for b in range(HB):
                    t0 = (s * HB + b) * S
                    mm = pe.matmul(pT[0:S, b * S:(b + 1) * S], cB[:, t0:t0 + S], cC[:, t0:t0 + S],
                                   start=True, stop=True)
                mm.then_inc(cb_mm, 1)

            def y_product(g, q, s):
                if s == 0:
                    pe.wait_ge(skip_done, g * KG + (q + 1))
                pe.wait_ge(m_done, g * (2 * KG) + (2 * q + s + 1))
                pe.wait_ge(hc_done, g * (2 * KG) + (2 * q + s + 2))
                for b in range(HB):
                    for hh in range(2):
                        mm = pe.matmul(pY[hh * HP:(hh + 1) * HP, s, b * S:(b + 1) * S],
                                       hc[:, s * HB + b, hh * HP:(hh + 1) * HP],
                                       m_t[q % 2][:, s * HB + b, hh, :], start=True, stop=True)
                mm.then_inc(y_mm, 1)

            def group(g):
                F = lambda f, *a: lambda: f(g, *a)
                project(g, 0, h, range(KD))
                project(g, 1, h, range(KD))
                for q in range(KG):
                    hf = {0: [F(seg, q, 0)], 2: [F(seg, q, 1)], 4: [F(seg, q, 2)], 6: [F(seg, q, 3)]}
                    if q == 0:
                        gf = {3: [F(cb, 0)], 7: [F(cb, 1)]}
                    else:
                        hf[1], hf[5] = [F(turn, q - 1, 0)], [F(turn, q - 1, 1)]
                        gf = {3: [F(y_product, q - 1, 0)], 5: [F(y_product, q - 1, 1)]}
                    project(g, 2 + 2 * q, h, range(KD), hf)
                    project(g, 3 + 2 * q, h, range(KD), gf)
                o0 = 2 + 2 * KG
                q = KG - 1

                def y_ready(k):
                    pe.wait_ge(y_done, g * KG + (k + 1))
                project(g, o0, y, range(KD - 1), {0: [F(turn, q, 0)], 4: [F(turn, q, 1)]}, last=False, gate_k=y_ready)
                project(g, o0 + 1, y, range(KD - 1), {3: [F(y_product, q, 0)], 4: [F(y_product, q, 1)]}, last=False)
                project(g, o0, y, [KD - 1], first=False, gate_k=y_ready)
                project(g, o0 + 1, y, [KD - 1], first=False)
                pe.wait_ge(sum_done, g * (KG - 1) + (KG - 1))
                for b in range(NB):
                    mm = pe.matmul(pS[0:S, b:b + 1], ssum[:, b * S:(b + 1) * S], ones[:, 0:1], start=True, stop=True)
                mm.then_inc(gn_mm, 1)
                for s in range(2):
                    pe.wait_ge(gn_diag, g * 2 + s + 1)
                    mm = pe.matmul(pY[:, s, 0:TH], ones[0:S, :], diag[0:S, s * TH:(s + 1) * TH], start=True, stop=True)
                mm.then_inc(gn_bc, 1)
                for o in range(2, KD):
                    project(g, o0 + o, y, range(KD))

            with pe.Fori(0, G) as g:
                group(g)

            def layer_norm_sums(n):
                if n == 1:
                    pe.wait_ge(out_added, ALL_OUT + KD)
                else:
                    pe.wait_ge(x2_done, NB)
                total(pY, acc, ln_sum)
                total(pA, y, ln_sum, ln_sq, n * KD + 1)

            layer_norm_sums(1)

            def scores(b):
                pe.wait_ge(ctx_in[b % 2], 32 * (b // 2 + 1))
                if b >= 2:
                    pe.wait_ge(ex_done, b - 1)
                for k in range(KD):
                    if b == 0:
                        pe.wait_ge(ln_out, KD + k + 1)
                    mm = pe.matmul([pT, pS][b % 2][0:S, 0:LK], h[:, k, b * S:(b + 1) * S], ctxt_sb[b % 2][:, k, :],
                                   start=(k == 0), stop=(k == KD - 1))
                mm.then_inc(sc_mm, 1)

            scores(0)
            for b in range(NB):
                if b + 1 < NB:
                    scores(b + 1)
                pe.wait_ge(pn_done, b + 1)
                if b >= 2:
                    pe.wait_ge(pt_copy, b - 1)
                for c in range(CK):
                    mm = pe.transpose(pA[0:LC, b % 2, c * S:(c + 1) * S], prob[b % 2][:, c * LC:(c + 1) * LC],
                                      ident[0:S, 0:S])
                mm.then_inc(pt_mm, 1)
                pe.wait_ge(pt_copy, b + 1)
                if b >= 2:
                    pe.wait_ge(x2_done, b - 1)
                for d in range(KD):
                    for c in range(CK):
                        mm = pe.matmul([pY, pB][b % 2][:, d // 4, (d % 4) * S:(d % 4 + 1) * S],
                                       ctxn_sb[b % 2][:, c, d * P:(d + 1) * P], prob_t[b % 2][:, c, :],
                                       start=(c == 0), stop=(c == CK - 1))
                mm.then_inc(xo_mm, 1)

            layer_norm_sums(2)
            pe.wait_ge(ffn_in, 16 * 5)
            pe.wait_ge(ln_out, 3 * KD)
            for b in range(NB):
                for k in range(KD):
                    mm = pe.matmul(pT[0:S, b * NE:(b + 1) * NE], h[:, k, b * S:(b + 1) * S], gw[:, k, :],
                                   start=(k == 0), stop=(k == KD - 1))
            mm.then_inc(r_mm, 1)
            pe.wait_ge(r_own, 4)
            for s in range(2):
                for b in range(HB):
                    mm = pe.transpose([pT, pS][s][0:NE, b * S:(b + 1) * S], route[:, s * HB + b, :], ident[0:S, 0:S])
            mm.then_inc(r_tr, 1)
            pe.wait_ge(r_copy, 1)
            for k in range(KD):
                if k >= 2:
                    pe.wait_ge(xs_done, k - 1)
                for s in range(2):
                    mm = pe.matmul(pAB[k % 2][:, s, 0:TH], isc[:, k * P:(k + 1) * P], route_t[:, s * TH:(s + 1) * TH],
                                   start=True, stop=True)
                mm.then_inc(is_mm, 1)
            pe.wait_ge(xs_done, KD)
            pe.wait_ge(sign_done, KD)
            for o in range(KD):
                if o >= 1:
                    pe.wait_ge(os_copy, o)
                for s in range(2):
                    mm = pe.matmul(pY[:, s, 0:TH], osc[:, o * P:(o + 1) * P], route_t[:, s * TH:(s + 1) * TH],
                                   start=True, stop=True)
                mm.then_inc(os_mm, 1)
                if o >= 2:
                    pe.wait_ge(f_scaled, o - 1)
                for s in range(2):
                    for k in range(KD):
                        mm = pe.matmul(pAB[o % 2][:, s, 0:TH], wff[:, k, o * P:(o + 1) * P],
                                       h[:, k, s * TH:(s + 1) * TH], start=(k == 0), stop=(k == KD - 1))
                mm.then_inc(f_mm, 1)

        @block.scalar
        def _(act):
            def squares(n):
                for k in range(KD):
                    act.wait_ge(ln_centre, n * KD + k + 1)
                    nc.scalar.activation(y[:, k, :], h[:, k, :], ACT.Square).then_inc(ln_sq, 1)

            squares(0)
            act.wait_ge(ln_var, 1)
            nc.scalar.activation(sq[:], sq[:], ACT.Sqrt).then_inc(ln_std, 1)
            act.wait_ge(ln_var, 2)
            nc.scalar.activation(rs[:], rs[:], ACT.Sqrt).then_inc(ln_std, 1)
            act.wait_ge(const_in, 16 * 10)
            nc.scalar.activation(hexp[:], hpar[:, 1:2], ACT.Exp).then_inc(dt_act, 1)
            act.wait_ge(dt_mm, 1)
            act.wait_ge(ln_out, KD)
            nc.scalar.activation(flat(th), halves(pB), ACT.Abs, bias=hpar[:, 0:1]).then_inc(dt_abs, 1)
            act.wait_ge(dt_abs, 1)
            nc.scalar.activation(th[:], th[:], ACT.Exp, scale=-1.0).then_inc(dt_act, 1)
            act.wait_ge(dt_act, 2)
            nc.scalar.activation(th[:], th[:], ACT.Ln, bias=1.0).then_inc(dt_act, 1)
            act.wait_ge(cs_split, 3)
            nc.scalar.mul(cs_parts(1), cs_parts(0), -1.0).then_inc(cs_negd, 1)

            act.wait_ge(halved, 1)

            def group(g):
                def conv_tanh(c, buf, t):
                    act.wait_ge(proj_done, g * TPG + (t + 1))
                    if c == 0:
                        act.wait_ge(yg_done, g * KG + 2)
                    elif c >= 2:
                        act.wait_ge(yg_done, g * KG + (c - 1))
                    w = par[:, bass.ds(g * CPG + c, 1), :].squeeze(1)
                    nc.scalar.activation(flat(buf), halves(pAB[t % 2]), ACT.Identity, bias=w[:, CONV:CONV + 1],
                                         scale=w[:, CONV - 1:CONV]).then_inc(conv_done, 1)
                    act.wait_ge(conv_done, g * (CST * CPG) + CST * (c + 1))
                    if c:
                        act.wait_ge(silu_done, g * CPG + c)
                    else:
                        act.wait_ge(out_added, g * KD + KD)
                    nc.scalar.activation(th[:], buf[:], ACT.Tanh).then_inc(tanh_c, 1)

                def gate_tanh(q):
                    act.wait_ge(proj_done, g * TPG + (4 + 2 * q))
                    nc.scalar.activation(flat(gate[q % 2]), halves(pB), ACT.Tanh, scale=0.5).then_inc(tanh_g, 1)

                def exps(q):
                    for n in range(4):
                        act.wait_ge(seg_mm, g * (4 * KG) + (4 * q + n + 1))
                        nc.scalar.activation(m_t[q % 2][:, 2 * n:2 * n + 2].rearrange("p b h i -> p (b h i)"),
                                             pS[0:S, 0:4 * S], ACT.Exp).then_inc(exp_done, 1)

                def y_out(q):
                    act.wait_ge(yg_done, g * KG + (q + 3))
                    w = par[:, bass.ds(g * CPG + (2 + q), 1), :].squeeze(1)
                    nc.scalar.activation(y[:, q, :], gate[q % 2][:], ACT.Copy, scale=w[:, NPAR - 1:NPAR])\
                        .then_inc(y_done, 1)
                    if q >= 2:
                        act.wait_ge(sum_done, g * (KG - 1) + (q - 1))
                    nc.scalar.activation(sq[:] if q else ssum, gate[q % 2][:], ACT.Square).then_inc(sq_done, 1)

                conv_tanh(0, cB, 0)
                conv_tanh(1, cC, 1)
                for q in range(KG):
                    if q:
                        gate_tanh(q - 1)
                    exps(q)
                    conv_tanh(2 + q, hid[q % 2], 2 + 2 * q)
                    if q:
                        y_out(q - 1)
                gate_tanh(KG - 1)
                y_out(KG - 1)
                act.wait_ge(gn_var, g + 1)
                nc.scalar.activation(small[:], small[:], ACT.Sqrt).then_inc(gn_std, 1)
                act.wait_ge(gn_bc, g + 1)
                nc.scalar.copy(flat(rs), halves(pY)).then_inc(gn_rs, 1)

            with act.Fori(0, G) as g:
                group(g)

            squares(1)
            act.wait_ge(ln_var, 3)
            nc.scalar.activation(ln_r[:], ln_r[:], ACT.Sqrt).then_inc(ln_std, 1)
            for b in range(NB):
                act.wait_ge(mx_done, b + 1)
                if b >= 2:
                    act.wait_ge(pt_mm, b - 1)
                nc.scalar.activation(prob[b % 2][:], [pT, pS][b % 2][0:S, 0:LK], ACT.Exp, bias=stat[:, 0, b:b + 1],
                                     accum_out=stat[:, 1, b:b + 1]).then_inc(ex_done, 1)
            act.wait_ge(ffn_in, 16 * 5)
            for k in range(KD):
                nc.scalar.activation(wff[:, k, :], wff[:, k, :], ACT.Sign).then_inc(sign_done, 1)
            squares(2)
            act.wait_ge(ln_var, 4)
            nc.scalar.activation(ln_r[:], ln_r[:], ACT.Sqrt).then_inc(ln_std, 1)
            act.wait_ge(r_own, 1)
            nc.scalar.activation(route[:], route[:], ACT.Exp).then_inc(r_exp, 1)
            for o in range(KD):
                act.wait_ge(os_mm, o + 1)
                if o >= 2:
                    act.wait_ge(f_done, 2 * (o - 1))
                nc.scalar.copy(flat(oscale[o % 2]), halves(pY)).then_inc(os_copy, 1)

        @block.gpsimd
        def _(pool):
            nc.gpsimd.memset(ones[:], 1.0).then_inc(ones_set, 1)
            for k in range(KD):
                pool.wait_ge(ln_tmp, k + 1)
                nc.gpsimd.tensor_tensor(acc[:, k, :], acc[:, k, :], [gate[0], gate[1]][k % 2][:], ALU.add)\
                    .then_inc(acc_ln, 1)

            def group(g):
                for q in range(1, KG):
                    pool.wait_ge(sq_done, g * KG + (q + 1))
                    if q >= 2:
                        pool.wait_ge(sum_done, g * (KG - 1) + (q - 1))
                    nc.gpsimd.tensor_tensor(ssum, ssum, sq[:], ALU.add).then_inc(sum_done, 1)
                for o in range(KD):
                    pool.wait_ge(out_scaled, g * KD + (KD + o + 1))
                    nc.gpsimd.tensor_tensor(acc[:, o, :], acc[:, o, :], tmp[o % 2][:], ALU.add).then_inc(out_added, 1)

            with pool.Fori(0, G) as g:
                group(g)

        @block.vector
        def _(v):
            stt = nc.vector.scalar_tensor_tensor
            tt = nc.vector.tensor_tensor
            ts = nc.vector.tensor_scalar

            def centre(n):
                v.wait_ge(ln_sum, 2 * n + 1)
                for k in range(KD):
                    stt(flat3(h, k), halves(pY), -1.0 / D, flat3(acc, k), ALU.mult, ALU.add).then_inc(ln_centre, 1)

            def flat3(buf, k):
                return buf[:, k, :].rearrange("p (s n) -> p s n", s=2)

            v.sem_inc(out_scaled, KD)
            v.sem_inc(out_added, KD)
            v.sem_inc(skip_done, 1)
            v.sem_inc(exp_done, 1)
            v.sem_inc(hc_done, 1)
            v.sem_inc(yg_done, 2)
            centre(0)
            v.wait_ge(ln_sum, 2)
            ts(flat(sq), halves(pA), 1.0 / D, EPS, ALU.mult, ALU.add).then_inc(ln_var, 1)
            v.wait_ge(ln_std, 1)
            nc.vector.reciprocal(th[:], sq[:]).then_inc(ln_own, 1)
            v.wait_ge(ln_own, 1)
            tt(cB[:], th[:], th[:], ALU.mult).then_inc(ln_own, 1)
            v.wait_ge(ln_own, 2)
            stt(flat(rs), halves(pA), 1.0 / D, flat(cB), ALU.mult, ALU.mult).then_inc(ln_own, 1)
            v.wait_ge(ln_own, 3)
            ts(rs[:], rs[:], EPS, None, ALU.add).then_inc(ln_var, 1)
            v.wait_ge(ln_std, 2)
            nc.vector.reciprocal(cB[:], rs[:]).then_inc(ln_own, 1)
            v.wait_ge(ln_own, 4)
            tt(hid[0][:], cB[:], th[:], ALU.mult).then_inc(ln_own, 1)
            v.wait_ge(ln_own, 5)
            v.wait_ge(const_in, 16 * 10)
            for k in range(KD):
                if k >= 2:
                    v.wait_ge(acc_ln, k - 1)
                tt([gate[0], gate[1]][k % 2][:], h[:, k, :], th[:], ALU.mult).then_inc(ln_tmp, 1)
                v.wait_ge(ln_tmp, k + 1)
                stt(h[:, k, :], h[:, k, :], nw[:, k:k + 1], hid[0][:], ALU.mult, ALU.mult).then_inc(ln_out, 1)
            ts(par[:, :, 0:CONV + 1], par[:, :, 0:CONV + 1], 0.5, None, ALU.mult).then_inc(dt_own, 1)
            ts(par[:, :, NPAR - 1:NPAR], par[:, :, NPAR - 1:NPAR], 0.5, None, ALU.mult).then_inc(halved, 1)

            v.wait_ge(dt_mm, 1)
            v.wait_ge(acc_ln, KD)
            v.wait_ge(dt_abs, 1)
            ts(flat(gate[0]), halves(pB), hpar[:, 0:1], 0.0, ALU.add, ALU.max).then_inc(dt_max, 1)
            v.wait_ge(dt_act, 3)
            v.wait_ge(dt_max, 1)
            tt(gate[0][:], gate[0][:], th[:], ALU.add).then_inc(dt_own, 1)
            v.wait_ge(dt_own, 2)
            ts(gate[1][:], gate[0][:], hexp[:, 0:1], -1.0, ALU.mult, ALU.mult).then_inc(dt_own, 1)
            for n in range(4):
                v.wait_ge(dt_tr, n + 1)
                src = [pT, pS][n % 2][0:S, :]
                dst = (dt_t[:].rearrange("p b h -> p (b h)") if n < 2
                       else m_t[0][:].rearrange("p b h i -> p (b h i)"))
                nc.vector.tensor_copy(dst[:, n % 2 * HB * P:(n % 2 + 1) * HB * P], src).then_inc(dt_copy, 1)
            v.wait_ge(cs_mm, 1)
            parts = [cs_parts(0)[:, c * T:(c + 1) * T] for c in range(3)]
            nc.vector.tensor_copy(flat(sq), halves(pY)).then_inc(dt_own, 1)
            v.wait_ge(dt_own, 4)
            nc.vector.tensor_copy(parts[0], sq[:]).then_inc(cs_split, 1)
            v.wait_ge(cs_split, 1)
            tt(sq[:], sq[:], parts[0], ALU.subtract).then_inc(dt_own, 1)
            v.wait_ge(dt_own, 5)
            nc.vector.tensor_copy(parts[1], sq[:]).then_inc(cs_split, 1)
            v.wait_ge(cs_split, 2)
            tt(sq[:], sq[:], parts[1], ALU.subtract).then_inc(dt_own, 1)
            v.wait_ge(dt_own, 6)
            nc.vector.tensor_copy(parts[2], sq[:]).then_inc(cs_split, 1)
            v.wait_ge(cs_negd, 1)
            v.wait_ge(halved, 1)

            def group(g):
                def taps(c, buf, t):
                    w = par[:, bass.ds(g * CPG + c, 1), :].squeeze(1)
                    for n in range(1, CONV):
                        for s in range(2):
                            v.wait_ge(conv_done, g * (CST * CPG) + (CST * c + (1 if n == 1 else 2 * n - 2 + s)))
                            stt(shifted(buf, n)[:, s], batches(pAB[t % 2])[:, s, :, 0:S - n],
                                w[:, CONV - 1 - n:CONV - n], shifted(buf, n)[:, s], ALU.mult, ALU.add)\
                                .then_inc(conv_done, 1)

                def silu(c, buf):
                    v.wait_ge(tanh_c, g * CPG + (c + 1))
                    stt(buf[:], th[:], 1.0, buf[:], ALU.add, ALU.mult).then_inc(silu_done, 1)

                def cb_out(s):
                    v.wait_ge(cb_mm, g * 2 + (s + 1))
                    nc.vector.tensor_copy(g_t[:, s * HB:(s + 1) * HB, :].rearrange("p b i -> p (b i)"),
                                          pT[0:S, 0:TH]).then_inc(cb_copy, 1)

                def gate_out(q):
                    v.wait_ge(tanh_g, g * KG + (q + 1))
                    stt(flat(gate[q % 2]), flat(gate[q % 2]), 1.0, halves(pB), ALU.add, ALU.mult).then_inc(gated, 1)

                def tokens_out(q, s):
                    v.wait_ge(tr_done, g * (2 * KG) + (2 * q + s + 1))
                    bs = slice(s * HB, (s + 1) * HB)
                    tt(hc[:, bs, :].rearrange("p b (h c) -> p b h c", h=2),
                       pT[0:S, :].rearrange("p (b h c) -> p b h c", b=HB, h=2),
                       bc(dt_t[:, bs, bass.ds(g * (2 * KG) + 2 * q, 2)].unsqueeze(3), [S, HB, 2, HP]),
                       ALU.mult).then_inc(hc_done, 1)

                def decay(q, s):
                    if q == 0 and s == 0:
                        v.wait_ge(cb_copy, g * 2 + 2)
                    v.wait_ge(exp_done, g * (4 * KG) + (4 * q + 2 * s + 3))
                    bs = slice(s * HB, (s + 1) * HB)
                    tt(m_t[q % 2][:, bs], m_t[q % 2][:, bs], bc(g_t[:, bs, :].unsqueeze(2), [S, HB, 2, S]),
                       ALU.mult).then_inc(m_done, 1)

                def skip(q):
                    v.wait_ge(y_mm, g * (2 * KG) + (2 * q + 2))
                    w = par[:, bass.ds(g * CPG + (2 + q), 1), :].squeeze(1)
                    stt(flat(hid[q % 2]), flat(hid[q % 2]), w[:, CONV + 1:CONV + 2], halves(pY), ALU.mult, ALU.add)\
                        .then_inc(skip_done, 1)

                def gate_y(q):
                    v.wait_ge(skip_done, g * KG + (q + 2))
                    tt(gate[q % 2][:], gate[q % 2][:], hid[q % 2][:], ALU.mult).then_inc(yg_done, 1)

                taps(0, cB, 0)
                silu(0, cB)
                taps(1, cC, 1)
                silu(1, cC)
                for q in range(KG + 1):
                    if q:
                        gate_out(q - 1)
                        tokens_out(q - 1, 0)
                        decay(q - 1, 0)
                        tokens_out(q - 1, 1)
                        decay(q - 1, 1)
                    if q < KG:
                        taps(2 + q, hid[q % 2], 2 + 2 * q)
                    if q:
                        skip(q - 1)
                    if q < KG:
                        silu(2 + q, hid[q % 2])
                    if q:
                        gate_y(q - 1)
                    if q == 0:
                        cb_out(0)
                        cb_out(1)
                v.wait_ge(gn_mm, g + 1)
                ts(small[:], pS[0:S, 0:NB], 0.25 / (DI // G), EPS, ALU.mult, ALU.add).then_inc(gn_var, 1)
                v.wait_ge(gn_std, g + 1)
                nc.vector.reciprocal(small[:], small[:]).then_inc(gn_r, 1)
                v.wait_ge(gn_r, g + 1)
                for s in range(2):
                    tt(diag[0:S, s * TH:(s + 1) * TH].rearrange("p (b i) -> p b i", b=HB),
                       bc(ident[0:S, 0:S].unsqueeze(1), [S, HB, S]),
                       bc(small[:, s * HB:(s + 1) * HB].unsqueeze(2), [S, HB, S]), ALU.mult).then_inc(gn_diag, 1)
                v.wait_ge(gn_rs, g + 1)
                for o in range(KD):
                    t = 2 + 2 * KG + o
                    v.wait_ge(proj_done, g * TPG + (t + 1))
                    if o >= 2:
                        v.wait_ge(out_added, g * KD + (KD + o - 1))
                    else:
                        v.wait_ge(sum_done, g * (KG - 1) + (KG - 1))
                    tt(flat(tmp[o % 2]), halves(pAB[t % 2]), flat(rs), ALU.mult).then_inc(out_scaled, 1)

            with v.Fori(0, G) as g:
                group(g)

            def layer_norm(n):
                centre(n)
                v.wait_ge(ln_sum, 2 * n + 2)
                ts(flat(ln_r), halves(pA), 1.0 / D, EPS, ALU.mult, ALU.add).then_inc(ln_var, 1)
                v.wait_ge(ln_std, 2 + n)
                nc.vector.reciprocal(oscale[0][:], ln_r[:]).then_inc(ln_own, 1)
                v.wait_ge(ln_own, 5 + n)
                for k in range(KD):
                    tt(h[:, k, :], h[:, k, :], oscale[0][:], ALU.mult).then_inc(ln_out, 1)

            layer_norm(1)
            for b in range(NB + 1):
                if b < NB:
                    ps = [pT, pS][b % 2]
                    v.wait_ge(sc_mm, b + 1)
                    nc.vector.tensor_reduce(stat[:, 3, b:b + 1], ps[0:S, 0:LK], AX.X, ALU.max).then_inc(sub_done, 1)
                    v.wait_ge(sub_done, 2 * b + 1)
                    ts(stat[:, 0, b:b + 1], stat[:, 3, b:b + 1], -1.0, None, ALU.mult).then_inc(mx_done, 1)
                    v.wait_ge(ex_done, b + 1)
                    nc.vector.reciprocal(stat[:, 2, b:b + 1], stat[:, 1, b:b + 1]).then_inc(sub_done, 1)
                    v.wait_ge(sub_done, 2 * b + 2)
                    ts(prob[b % 2][:], prob[b % 2][:], stat[:, 2, b:b + 1], None, ALU.mult).then_inc(pn_done, 1)
                    v.wait_ge(pt_mm, b + 1)
                    nc.vector.tensor_copy(prob_t[b % 2][:].rearrange("p c i -> p (c i)"), pA[0:LC, b % 2, 0:CK * S])\
                        .then_inc(pt_copy, 1)
                if b:
                    c = b - 1
                    v.wait_ge(xo_mm, c + 1)
                    xa = acc[:, :, c * S:(c + 1) * S].rearrange("p (s d) i -> p s d i", s=2)
                    tt(xa, batches([pY, pB][c % 2]), xa, ALU.add).then_inc(x2_done, 1)

            v.wait_ge(x2_done, NB)
            layer_norm(2)
            v.wait_ge(r_mm, 1)
            logits = pT[0:S, 0:NB * NE].rearrange("p (b e) -> p b e", b=NB)
            nc.vector.tensor_reduce(rstat[:, 0, :], logits, AX.X, ALU.max).then_inc(sub_done, 1)
            v.wait_ge(sub_done, 2 * NB + 1)
            tt(route[:], logits, bc(rstat[:, 0, :].unsqueeze(2), [S, NB, NE]), ALU.subtract).then_inc(r_own, 1)
            v.wait_ge(r_exp, 1)
            nc.vector.tensor_reduce(rstat[:, 1, :], route[:], AX.X, ALU.add).then_inc(r_own, 1)
            v.wait_ge(r_own, 2)
            nc.vector.reciprocal(rstat[:, 0, :], rstat[:, 1, :]).then_inc(r_own, 1)
            v.wait_ge(r_own, 3)
            tt(route[:], route[:], bc(rstat[:, 0, :].unsqueeze(2), [S, NB, NE]), ALU.mult).then_inc(r_own, 1)
            v.wait_ge(r_tr, 1)
            nc.vector.tensor_copy(route_t[:, 0:TH], pT[0:NE, 0:TH]).then_inc(sub_done, 1)
            nc.vector.tensor_copy(route_t[:, TH:T], pS[0:NE, 0:TH]).then_inc(r_copy, 1)
            for k in range(KD):
                v.wait_ge(is_mm, k + 1)
                tt(flat3(h, k), flat3(h, k), halves(pAB[k % 2]), ALU.mult).then_inc(xs_done, 1)
            for o in range(KD):
                v.wait_ge(f_mm, o + 1)
                v.wait_ge(os_copy, o + 1)
                tt(flat(oscale[o % 2]), halves(pAB[o % 2]), flat(oscale[o % 2]), ALU.mult).then_inc(f_scaled, 1)
                v.wait_ge(f_scaled, o + 1)
                for s in range(2):
                    cols = slice(s * TH, (s + 1) * TH)
                    stt(acc[:, o, cols], oscale[o % 2][:, cols], fb[:, o:o + 1], acc[:, o, cols], ALU.add, ALU.add)\
                        .then_inc(f_done, 1)


def kernel(**inputs):
    import ml_dtypes
    import concourse.bacc as bacc
    from concourse.bass_utils import run_bass_kernel_spmd as run

    A = {k: np.asarray(v) for k, v in inputs.items()}
    L = "L0_attn_"

    def channels(v):
        return np.moveaxis(v.reshape(-1, P, *v.shape[1:]), 1, 0)

    w_in = A[L + "in_proj_w"].reshape(-1, P, KD, P).transpose(0, 3, 2, 1)
    w_out = A[L + "out_proj_w"].reshape(KD, P, G, KG, P).transpose(2, 0, 4, 3, 1)
    n_di = DI // P
    order = []
    for g in range(G):
        tiles = [w_in[2 * n_di + g], w_in[2 * n_di + G + g]]
        for q in range(KG):
            tiles += [w_in[n_di + g * KG + q], w_in[g * KG + q]]
        order += tiles + [w_out[g, o] for o in range(KD)]
    conv_w, conv_b = A[L + "conv_w"], A[L + "conv_b"]
    skip = np.repeat(A[L + "Dp"], HP)
    par_c = np.zeros((conv_w.shape[0], NPAR), np.float32)
    par_c[:, 0:CONV], par_c[:, CONV] = conv_w, conv_b
    par_c[:DI, CONV + 1], par_c[:DI, CONV + 2] = skip, A[L + "gnorm_w"]
    par_t = par_c.reshape(-1, P, NPAR)
    par = np.stack([par_t[t] for g in range(G) for t in [n_di + g, n_di + G + g] + list(range(g * KG, (g + 1) * KG))], 1)

    const32 = np.zeros((P, P + S), np.float32)
    const32[:, :P] = np.eye(P)
    const32[:S, P:] = np.triu(np.ones((S, S)))
    bf = ml_dtypes.bfloat16
    mask = np.zeros((S, 5, S), np.float32)
    mask[:, 0:4] = np.where(np.arange(S)[None, :] < np.arange(S)[:, None], MASKED, 0.0)[:, None, :]
    mask[:, 4] = np.eye(S)
    seg_r0 = np.zeros((SEGK, NB, 2, S), np.float32)
    seg_r0[3:6, :, 0], seg_r0[6:9, :, 1] = 1, 1
    seg_l0 = np.zeros((SEGK, NB, S), np.float32)
    seg_l0[0:3] = 1

    arrays = {
        "x_t": A["x"].reshape(T, D).T,
        "w_dt": w_in[-1],
        "w_main": np.stack(order),
        "par": par,
        "norm_w": channels(A[L + "norm_w"]),
        "head_par": np.stack([A[L + "dt_bias"], A[L + "A_log"]], 1),
        "const32": const32,
        "mask": mask.astype(bf),
        "seg_r0": seg_r0.astype(bf),
        "seg_l0": seg_l0.astype(bf),
        "ctx_t": A["ctx_4096"].transpose(0, 2, 1),
        "ctx_n": A["ctx_4096"],
        "w_ffn": A["L0_ffn_weight"].reshape(D, KD, P).transpose(2, 1, 0),
        "gate_w": A["L0_ffn_gate_w"].T,
        "in_scale": A["L0_ffn_in_channel_scale"],
        "out_scale": A["L0_ffn_out_channel_scale"],
        "ffn_bias": channels(A["L0_ffn_bias"]),
    }
    arrays = {k: np.ascontiguousarray(v) for k, v in arrays.items()}
    nc = bacc.Bacc("TRN2", target_bir_lowering=False, num_devices=1)
    arrays = {f"in_{k}": v for k, v in arrays.items()}
    args = [nc.dram_tensor(k, v.shape, mybir.dt.from_np(v.dtype), kind="ExternalInput").ap() for k, v in arrays.items()]
    out = nc.dram_tensor("out_t", (D, T), F32, kind="ExternalOutput").ap()
    build(nc, *args, out)
    r = run(nc, [arrays], core_ids=[0])
    return np.ascontiguousarray(r.results[0]["out_t"].T).reshape(NB, S, D)
```

```python
from contextlib import ExitStack

import numpy as np

import concourse.bass as bass
from concourse import mybir

F32 = mybir.dt.float32
BF16 = mybir.dt.bfloat16
F32R = mybir.dt.float32r
ALU = mybir.AluOpType
ACT = mybir.ActivationFunctionType
AX = mybir.AxisListType

P = 128
NB, S, D = 8, 112, 1024
T = NB * S
TH = T // 2
HB = NB // 2
KD = D // P
HEADS, HP, G = 128, 64, 8
DI = HEADS * HP
KG = DI // G // P
TPG = 2 + 2 * KG + KD
CONV = 4
CST = 1 + 2 * (CONV - 1)
CPG = 2 + KG
NPAR = CONV + 3
EPS = 1e-5
LK, CK = 375, 3
LC = LK // CK
NE = 8
MASKED = -1e30
SEGK = 9


def bc(ap, shape):
    return ap.broadcast_to(shape)


def build(nc, x_t, w_main, par_d, norm_w, head_par, const32, mask_d, seg_r0, seg_l0, ctx_t, ctx_n,
          w_ffn, gate_w, in_scale, out_scale, ffn_bias, out):
    with ExitStack() as ctx:
        def sb(name, shape, dt=F32, scope=ctx):
            return scope.enter_context(nc.sbuf_tensor(name, shape, dt))

        def sem(name):
            return ctx.enter_context(nc.semaphore(name))

        pA = ctx.enter_context(nc.psum_tensor("pA", [P, 2, 512], F32))
        pB = ctx.enter_context(nc.psum_tensor("pB", [P, 2, 512], F32))
        pY = ctx.enter_context(nc.psum_tensor("pY", [P, 2, 512], F32))
        pT = ctx.enter_context(nc.psum_tensor("pT", [P, 512], F32))
        pS = ctx.enter_context(nc.psum_tensor("pS", [P, 512], F32))
        pAB = [pA, pB]

        def halves(ps):
            return ps[:, :, 0:TH]

        def batches(ps):
            return ps[:, :, 0:TH].rearrange("p s (b i) -> p s b i", b=HB)

        acc = sb("acc", [P, KD, T])
        ident = sb("ident", [P, P])
        ones = sb("ones", [P, P])

        mixer = ExitStack()
        h_hi = sb("h_hi", [P, KD, T], F32R, scope=mixer)
        h_lo = sb("h_lo", [P, KD, T], F32R, scope=mixer)
        w_raw = [sb(f"w_raw{i}", [P, KD, P], scope=mixer) for i in range(2)]
        w_hi = [sb(f"w_hi{i}", [P, KD, P], F32R, scope=mixer) for i in range(2)]
        w_lo = [sb(f"w_lo{i}", [P, KD, P], F32R, scope=mixer) for i in range(2)]
        start = ExitStack()
        xc = sb("xc", [P, KD, T], scope=start)
        x_sq = sb("x_sq", [P, KD, T], scope=start)
        start.close()
        y_hi = sb("y_hi", [P, KG, T], F32R, scope=mixer)
        y_lo = sb("y_lo", [P, KG, T], F32R, scope=mixer)
        par = sb("par", [P, G * CPG, NPAR], scope=mixer)
        nw = sb("nw", [P, KD], scope=mixer)
        hpar = sb("hpar", [P, 2], scope=mixer)
        hexp = sb("hexp", [P, 1], scope=mixer)
        tri = sb("tri", [S, S], scope=mixer)
        mask = sb("mask", [S, 5, S], BF16, scope=mixer)
        seg_r = [sb(f"seg_r{i}", [SEGK, HB, 2, S], BF16, scope=mixer) for i in range(2)]
        seg_l = [sb(f"seg_l{i}", [SEGK, HB, S], BF16, scope=mixer) for i in range(2)]
        dt_g = sb("dt_g", [S, NB, 2 * KG], scope=mixer)
        hid = sb("hid", [P, T], scope=mixer)
        gate = sb("gate", [P, T], scope=mixer)
        th = sb("th", [P, T], scope=mixer)
        hc = sb("hc", [S, NB, P], scope=mixer)
        m_t = sb("m_t", [P, NB, 2, S], scope=mixer)
        g_t = sb("g_t", [S, NB, S], scope=mixer)
        sq = sb("sq", [P, T], scope=mixer)
        ssum = sb("ssum", [P, T], scope=mixer)
        small = sb("small", [S, NB], scope=mixer)
        tmp = [sq, th]
        diag, rs = hid, gate
        m_flat = m_t[:].rearrange("p b h i -> p (b h i)")
        cB, cC = m_flat[:, 0:T], m_flat[:, T:2 * T]
        mixer.close()

        tail = ExitStack()
        h = sb("h", [P, KD, T], scope=tail)
        y = sb("y", [P, KD, T], scope=tail)
        ctxt_sb = [sb(f"ctxt_sb{i}", [P, KD, LK], scope=tail) for i in range(2)]
        ctxn_sb = [sb(f"ctxn_sb{i}", [LC, CK, D], scope=tail) for i in range(2)]
        wff = sb("wff", [P, KD, D], scope=tail)
        prob = [sb(f"prob{i}", [S, LK], scope=tail) for i in range(2)]
        prob_t = [sb(f"prob_t{i}", [LC, CK, S], scope=tail) for i in range(2)]
        stat = sb("stat", [S, 4, NB], scope=tail)
        ln_r = sb("ln_r", [P, T], scope=tail)
        gw = sb("gw", [P, KD, NE], scope=tail)
        isc = sb("isc", [NE, D], scope=tail)
        osc = sb("osc", [NE, D], scope=tail)
        fb = sb("fb", [P, KD], scope=tail)
        route = sb("route", [S, NB, NE], scope=tail)
        route_t = sb("route_t", [NE, T], scope=tail)
        rstat = sb("rstat", [S, 2, NB], scope=tail)
        oscale = [sb(f"oscale{i}", [P, T], scope=tail) for i in range(2)]
        tail.close()

        cs_pos = nc.dram_tensor("cs_pos", (HEADS, 3, T), BF16).ap()
        cs_neg = nc.dram_tensor("cs_neg", (HEADS, 3, T), BF16).ap()
        dt_dram = nc.dram_tensor("dt_dram", (G, S, NB, 2 * KG), F32).ap()

        x_in = sem("x_in")
        const_in = sem("const_in")
        w_in = [sem(f"w_in{i}") for i in range(2)]
        w_hi_done, w_lo_done = sem("w_hi_done"), sem("w_lo_done")
        h_hi_done, h_lo_done = sem("h_hi_done"), sem("h_lo_done")
        dt_in, yl_done = sem("dt_in"), sem("yl_done")
        seg_in = [sem(f"seg_in{i}") for i in range(2)]
        cs_out = sem("cs_out")
        ln_sum, ln_centre, ln_sq, ln_var, ln_std, ln_out, ln_own = (
            sem(x) for x in ("ln_sum", "ln_centre", "ln_sq", "ln_var", "ln_std", "ln_out", "ln_own"))
        ones_set = sem("ones_set")
        ln_tmp, acc_ln = sem("ln_tmp"), sem("acc_ln")
        dt_mm, dt_abs, dt_max, dt_act, dt_own, dt_tr, dt_copy, cs_mm, cs_split, cs_negd = (
            sem(x) for x in ("dt_mm", "dt_abs", "dt_max", "dt_act", "dt_own", "dt_tr", "dt_copy", "cs_mm", "cs_split", "cs_negd"))
        halved = sem("halved")
        proj_done = sem("proj_done")
        conv_done = sem("conv_done")
        tanh_c, silu_done = sem("tanh_c"), sem("silu_done")
        tanh_g, gated = sem("tanh_g"), sem("gated")
        seg_mm, exp_done = sem("seg_mm"), sem("exp_done")
        cb_mm, cb_copy = sem("cb_mm"), sem("cb_copy")
        tr_done, hc_done = sem("tr_done"), sem("hc_done")
        m_done = sem("m_done")
        y_mm, skip_done, yg_done, y_done, sq_done, sum_done = (
            sem(x) for x in ("y_mm", "skip_done", "yg_done", "y_done", "sq_done", "sum_done"))
        gn_mm, gn_var, gn_std, gn_r, gn_diag, gn_bc, gn_rs = (
            sem(x) for x in ("gn_mm", "gn_var", "gn_std", "gn_r", "gn_diag", "gn_bc", "gn_rs"))
        out_scaled, out_added = sem("out_scaled"), sem("out_added")
        ctx_in = [sem(f"ctx_in{i}") for i in range(2)]
        ffn_in = sem("ffn_in")
        sc_mm, mx_done, ex_done, ri_done, pn_done, pt_mm, pt_copy, xo_mm, x2_done, sub_done = (
            sem(x) for x in ("sc_mm", "mx_done", "ex_done", "ri_done", "pn_done", "pt_mm", "pt_copy", "xo_mm", "x2_done", "sub_done"))
        sign_done = sem("sign_done")
        r_mm, r_own, r_exp, r_tr, r_copy = (sem(x) for x in ("r_mm", "r_own", "r_exp", "r_tr", "r_copy"))
        is_mm, xs_done, f_mm, os_mm, os_copy, f_scaled, f_done, stored = (
            sem(x) for x in ("is_mm", "xs_done", "f_mm", "os_mm", "os_copy", "f_scaled", "f_done", "stored"))

        dt_tok = hc

        def bank(t):
            o = t - (2 + 2 * KG)
            return [pA, pB, pY][o % 3] if o >= 0 else [pA, pB][t % 2]

        ALL_OUT = G * KD

        block = ctx.enter_context(nc.Block())

        def da_t(b):
            return m_flat[0:S, b * HEADS:(b + 1) * HEADS]

        def cs_parts(i):
            return x_sq[:].rearrange("p k t -> p (k t)").bitcast(BF16)[:, i * 3 * T:(i + 1) * 3 * T]

        def flat(buf):
            return buf[:, :].rearrange("p (s n) -> p s n", s=2)

        def shifted(buf, n):
            return buf[:, :].rearrange("p (s b i) -> p s b i", s=2, b=HB)[:, :, :, n:S]

        @block.sync
        def _(sp):
            for i in range(2):
                k = slice(i * KD // 2, (i + 1) * KD // 2)
                sp.dma_start(acc[:, k, :], x_t.rearrange("(k p) t -> p k t", p=P)[:, k, :]).then_inc(x_in, 16)
            sp.dma_start(ident[:], const32[:, 0:P]).then_inc(const_in, 16)
            sp.dma_start(tri[:], const32[0:S, P:P + S]).then_inc(const_in, 16)
            sp.dma_start(nw[:], norm_w).then_inc(const_in, 16)
            sp.dma_start(hpar[:], head_par).then_inc(const_in, 16)
            sp.dma_start(par[:], par_d).then_inc(const_in, 16)
            sp.dma_start(mask[:], mask_d).then_inc(const_in, 16)

            def load_w(n, slot):
                sp.dma_start(w_raw[slot][:], w_main[n]).then_inc(w_in[slot], 16)

            load_w(0, 0)
            load_w(1, 1)
            for i in range(2):
                sp.dma_start(seg_r[i][:], seg_r0).then_inc(const_in, 16)
                sp.dma_start(seg_l[i][:], seg_l0).then_inc(const_in, 16)
            sp.wait_ge(dt_copy, 2)
            for g in range(G):
                sp.dma_start(dt_dram[g], dt_tok[:, :, g * 2 * KG:(g + 1) * 2 * KG]).then_inc(cs_out, 16)
            sp.wait_ge(cs_split, 3)
            sp.dma_start(cs_pos.rearrange("h c t -> h (c t)"), cs_parts(0)).then_inc(cs_out, 16)
            sp.wait_ge(cs_negd, 1)
            sp.dma_start(cs_neg.rearrange("h c t -> h (c t)"), cs_parts(1)).then_inc(cs_out, 16)
            sp.wait_ge(cs_out, 16 * (G + 2))
            sp.wait_ge(const_in, 16 * 10)

            def load_seg(g, q):
                sp.wait_ge(seg_mm, g * (4 * KG) + (4 * q + 1))
                heads = bass.ds(g * (2 * KG) + 2 * q, 2)
                pos = cs_pos[heads].rearrange("h c (s b i) -> c s b h i", s=2, b=HB)
                neg = cs_neg[heads].rearrange("h c (s b i) -> (h c) s b i", s=2, b=HB)
                for s in range(2):
                    for hh in range(2):
                        sp.dma_start(seg_r[s][0:3, :, hh, :], pos[:, s, :, hh, :]).then_inc(seg_in[s], 16)
                    sp.dma_start(seg_l[s][3:SEGK], neg[:, s]).then_inc(seg_in[s], 16)

            with sp.Fori(0, G) as g:
                for j in range(TPG):
                    sp.wait_ge(w_lo_done, g * TPG + (j + 1))
                    sp.dma_start(w_raw[j % 2][:], w_main[bass.ds(g * TPG + (j + 2), 1)].squeeze(0))\
                        .then_inc(w_in[j % 2], 16)
                    if j == 0:
                        sp.wait_ge(hc_done, g * (2 * KG) + 1)
                        sp.dma_start(dt_g[:], dt_dram[bass.ds(g, 1)].squeeze(0)).then_inc(dt_in, 16)
                    if j == 1:
                        load_seg(g, 0)
                    if j >= 6 and j % 2 == 0 and j < 4 + 2 * KG:
                        load_seg(g, (j - 4) // 2)

            sp.wait_ge(out_added, ALL_OUT + KD)
            for b in range(NB):
                if b >= 2:
                    sp.wait_ge(xo_mm, b - 1)
                sp.dma_start(ctxt_sb[b % 2][:], ctx_t[b].rearrange("(k p) n -> p k n", p=P)).then_inc(ctx_in[b % 2], 16)
                sp.dma_start(ctxn_sb[b % 2][:], ctx_n[b].rearrange("(k p) n -> p k n", p=LC)).then_inc(ctx_in[b % 2], 16)
                if b == 1:
                    sp.dma_start(gw[:], gate_w.rearrange("(k p) e -> p k e", p=P)).then_inc(ffn_in, 16)
                    sp.dma_start(isc[:], in_scale).then_inc(ffn_in, 16)
                    sp.dma_start(osc[:], out_scale).then_inc(ffn_in, 16)
                    sp.dma_start(fb[:], ffn_bias).then_inc(ffn_in, 16)
                    sp.dma_start(wff[:], w_ffn).then_inc(ffn_in, 16)
            for o in range(KD):
                sp.wait_ge(f_done, 2 * o + 2)
                sp.dma_start(out[o * P:(o + 1) * P, :], acc[:, o, :]).then_inc(stored, 16)
            sp.wait_ge(stored, 16 * KD)

        @block.tensor
        def _(pe):
            def total(ps, src, done, value_sem=None, value=0):
                for s in range(2):
                    for k in range(KD):
                        if s == 0 and value_sem is not None:
                            pe.wait_ge(value_sem, value + k)
                        mm = pe.matmul(ps[:, s, 0:TH], ones[:], src[:, k, s * TH:(s + 1) * TH],
                                       start=(k == 0), stop=(k == KD - 1))
                mm.then_inc(done, 1)

            pe.wait_ge(x_in, 32)
            pe.wait_ge(ones_set, 1)
            total(pY, acc, ln_sum)
            total(pA, x_sq, ln_sum, ln_sq, 1)

            def products(ps, n_slot, r_hi, r_lo, k):
                passes = [(w_hi, r_hi), (w_hi, r_lo), (w_lo, r_hi)]
                for i, (w, r) in enumerate(passes):
                    for s in range(2):
                        mm = pe.matmul(ps[:, s, 0:TH], w[n_slot][:, k, :], r[:, k, s * TH:(s + 1) * TH],
                                       start=(k == 0 and i == 0), stop=(k == KD - 1 and i == 2))
                return mm

            pe.wait_ge(w_lo_done, 1)
            for k in range(KD):
                pe.wait_ge(h_lo_done, k + 1)
                mm = products(pB, 0, h_hi, h_lo, k)
            mm.then_inc(proj_done, 1)
            pe.wait_ge(const_in, 16 * 10)
            for n in range(4):
                pe.wait_ge(dt_own, 2 + n // 2)
                if n >= 2:
                    pe.wait_ge(dt_copy, n - 1)
                src = [gate, hid][n // 2]
                for b in range(HB):
                    t0 = (n % 2 * HB + b) * S
                    mm = pe.transpose([pT, pS][n % 2][0:S, b * P:(b + 1) * P], src[:, t0:t0 + S], ident[:])
                mm.then_inc(dt_tr, 1)
            pe.wait_ge(dt_copy, 4)
            for b in range(NB):
                mm = pe.matmul(pY[:, b // HB, (b % HB) * S:(b % HB + 1) * S], da_t(b), tri[:],
                               start=True, stop=True)
            mm.then_inc(cs_mm, 1)

            def project(g, t, r_hi, r_lo, ks, fillers=None, before=None):
                if 0 in ks:
                    pe.wait_ge(w_lo_done, g * TPG + (t + 2))
                    free_bank(g, t)
                for k in ks:
                    if before is not None:
                        before(k)
                    mm = products(bank(t), (t + 1) % 2, r_hi, r_lo, k)
                    if k == KD - 1:
                        mm.then_inc(proj_done, 1)
                    for f in (fillers or {}).get(k, []):
                        f()

            def free_bank(g, t):
                o = t - (2 + 2 * KG)
                if t < 2:
                    pe.wait_ge(out_scaled, g * KD + (KD - 1 + t))
                elif t < 4:
                    pe.wait_ge(conv_done, g * (CST * CPG) + CST * (t - 1))
                elif t % 2 == 0 and o <= 0:
                    pe.wait_ge(conv_done, g * (CST * CPG) + CST * (t // 2 + 1))
                elif o <= 1:
                    pe.wait_ge(gated, g * KG + (t - 3) // 2)
                elif o == 2:
                    pe.wait_ge(skip_done, g * KG + (KG + 1))
                else:
                    pe.wait_ge(out_scaled, g * KD + (KD + o - 2))

            def seg(g, q, n):
                s = n // 2
                if n % 2 == 0:
                    pe.wait_ge(seg_in[s], g * (48 * KG) + 48 * (q + 1))
                pe.wait_ge(exp_done, g * (4 * KG) + (4 * q + n + 1))
                pe.matmul(pS[0:S, 0:4 * S], mask[:, 4, :], mask[:, 0:4, :], start=True, stop=False,
                          skip_group_check=True)
                for j in range(2):
                    b = n % 2 * 2 + j
                    mm = pe.matmul(pS[0:S, 2 * j * S:2 * (j + 1) * S], seg_l[s][:, b, :], seg_r[s][:, b, :, :],
                                   start=False, stop=(j == 1), skip_group_check=True)
                mm.then_inc(seg_mm, 1)

            def turn(g, q, s):
                if s == 0:
                    pe.wait_ge(silu_done, g * CPG + (q + 3))
                    if q == 0:
                        pe.wait_ge(cb_copy, g * 2 + 2)
                    else:
                        pe.wait_ge(hc_done, g * (2 * KG) + (2 * q + 1))
                else:
                    pe.wait_ge(hc_done, g * (2 * KG) + (2 * q + 2))
                for b in range(HB):
                    t0 = (s * HB + b) * S
                    mm = pe.transpose(pT[0:S, b * P:(b + 1) * P], hid[:, t0:t0 + S], ident[:])
                mm.then_inc(tr_done, 1)

            def cb(g, s):
                pe.wait_ge(silu_done, g * CPG + 2)
                if s == 0:
                    pe.wait_ge(hc_done, g * (2 * KG) + 1)
                else:
                    pe.wait_ge(cb_copy, g * 2 + 1)
                for b in range(HB):
                    t0 = (s * HB + b) * S
                    mm = pe.matmul(pT[0:S, b * S:(b + 1) * S], cB[:, t0:t0 + S], cC[:, t0:t0 + S],
                                   start=True, stop=True)
                mm.then_inc(cb_mm, 1)

            def y_product(g, q, s):
                if s == 0:
                    pe.wait_ge(skip_done, g * KG + (q + 1))
                pe.wait_ge(m_done, g * (2 * KG) + (2 * q + s + 1))
                pe.wait_ge(hc_done, g * (2 * KG) + (2 * q + s + 2))
                for b in range(HB):
                    for hh in range(2):
                        mm = pe.matmul(pY[hh * HP:(hh + 1) * HP, s, b * S:(b + 1) * S],
                                       hc[:, s * HB + b, hh * HP:(hh + 1) * HP],
                                       m_t[0:S, s * HB + b, hh, :], start=True, stop=True)
                mm.then_inc(y_mm, 1)

            def group(g):
                F = lambda f, *a: lambda: f(g, *a)
                w, yk = (h_hi, h_lo), (y_hi, y_lo)
                project(g, 0, *w, range(KD))
                project(g, 1, *w, range(KD))
                for q in range(KG):
                    if q == 0:
                        hf = {6: [F(cb, 0)]}
                        gf = {0: [F(cb, 1)], 1: [F(seg, q, 0)], 3: [F(seg, q, 1)], 5: [F(seg, q, 2)], 6: [F(seg, q, 3)]}
                    else:
                        hf = {0: [F(turn, q - 1, 0)], 2: [F(turn, q - 1, 1)],
                              4: [F(y_product, q - 1, 0)], 5: [F(y_product, q - 1, 1)]}
                        gf = {0: [F(seg, q, 0)], 2: [F(seg, q, 1)], 4: [F(seg, q, 2)], 6: [F(seg, q, 3)]}
                    project(g, 2 + 2 * q, *w, range(KD), hf)
                    project(g, 3 + 2 * q, *w, range(KD), gf)
                o0 = 2 + 2 * KG
                q = KG - 1

                def y_ready(k):
                    pe.wait_ge(yl_done, g * KG + (k + 1))
                project(g, o0, *yk, range(KD - 1), {0: [F(turn, q, 0)], 2: [F(turn, q, 1)],
                                                    4: [F(y_product, q, 0)], 5: [F(y_product, q, 1)]}, y_ready)
                project(g, o0 + 1, *yk, range(4))
                project(g, o0, *yk, [KD - 1], before=y_ready)
                project(g, o0 + 1, *yk, range(4, KD))

                def gn_sums():
                    pe.wait_ge(sum_done, g * (KG - 1) + (KG - 1))
                    for b in range(NB):
                        mm = pe.matmul(pS[0:S, b:b + 1], ssum[:, b * S:(b + 1) * S], ones[:, 0:1],
                                       start=True, stop=True)
                    mm.then_inc(gn_mm, 1)

                def gn_spread():
                    for s in range(2):
                        pe.wait_ge(gn_diag, g * 2 + s + 1)
                        mm = pe.matmul([pT, pS][s][:, 0:TH], ones[0:S, :], diag[0:S, s * TH:(s + 1) * TH],
                                       start=True, stop=True)
                    mm.then_inc(gn_bc, 1)
                for o in range(2, KD):
                    project(g, o0 + o, *yk, range(KD), {0: [gn_sums], 5: [gn_spread]} if o == 2 else None)

            with pe.Fori(0, G) as g:
                group(g)

            def layer_norm_sums(n):
                if n == 1:
                    pe.wait_ge(out_added, ALL_OUT + KD)
                else:
                    pe.wait_ge(x2_done, NB)
                total(pY, acc, ln_sum)
                total(pA, y, ln_sum, ln_sq, n * KD + 1)

            layer_norm_sums(1)

            def scores(b):
                pe.wait_ge(ctx_in[b % 2], 32 * (b // 2 + 1))
                if b >= 2:
                    pe.wait_ge(ex_done, b - 1)
                for k in range(KD):
                    if b == 0:
                        pe.wait_ge(ln_out, KD + k + 1)
                    mm = pe.matmul([pT, pS][b % 2][0:S, 0:LK], h[:, k, b * S:(b + 1) * S], ctxt_sb[b % 2][:, k, :],
                                   start=(k == 0), stop=(k == KD - 1))
                mm.then_inc(sc_mm, 1)

            scores(0)
            for b in range(NB):
                if b + 1 < NB:
                    scores(b + 1)
                pe.wait_ge(pn_done, b + 1)
                if b >= 2:
                    pe.wait_ge(pt_copy, b - 1)
                for c in range(CK):
                    mm = pe.transpose(pA[0:LC, b % 2, c * S:(c + 1) * S], prob[b % 2][:, c * LC:(c + 1) * LC],
                                      ident[0:S, 0:S])
                mm.then_inc(pt_mm, 1)
                pe.wait_ge(pt_copy, b + 1)
                if b >= 2:
                    pe.wait_ge(x2_done, b - 1)
                for d in range(KD):
                    for c in range(CK):
                        mm = pe.matmul([pY, pB][b % 2][:, d // 4, (d % 4) * S:(d % 4 + 1) * S],
                                       ctxn_sb[b % 2][:, c, d * P:(d + 1) * P], prob_t[b % 2][:, c, :],
                                       start=(c == 0), stop=(c == CK - 1))
                mm.then_inc(xo_mm, 1)

            layer_norm_sums(2)
            pe.wait_ge(ffn_in, 16 * 5)
            pe.wait_ge(ln_out, 3 * KD)
            for b in range(NB):
                for k in range(KD):
                    mm = pe.matmul(pT[0:S, b * NE:(b + 1) * NE], h[:, k, b * S:(b + 1) * S], gw[:, k, :],
                                   start=(k == 0), stop=(k == KD - 1))
            mm.then_inc(r_mm, 1)
            pe.wait_ge(r_own, 4)
            for s in range(2):
                for b in range(HB):
                    mm = pe.transpose([pT, pS][s][0:NE, b * S:(b + 1) * S], route[:, s * HB + b, :], ident[0:S, 0:S])
            mm.then_inc(r_tr, 1)
            pe.wait_ge(r_copy, 1)
            for k in range(KD):
                if k >= 2:
                    pe.wait_ge(xs_done, k - 1)
                for s in range(2):
                    mm = pe.matmul(pAB[k % 2][:, s, 0:TH], isc[:, k * P:(k + 1) * P], route_t[:, s * TH:(s + 1) * TH],
                                   start=True, stop=True)
                mm.then_inc(is_mm, 1)
            pe.wait_ge(xs_done, KD)
            pe.wait_ge(sign_done, KD)
            for o in range(KD):
                if o >= 1:
                    pe.wait_ge(os_copy, o)
                for s in range(2):
                    mm = pe.matmul(pY[:, s, 0:TH], osc[:, o * P:(o + 1) * P], route_t[:, s * TH:(s + 1) * TH],
                                   start=True, stop=True)
                mm.then_inc(os_mm, 1)
                if o >= 2:
                    pe.wait_ge(f_scaled, o - 1)
                for s in range(2):
                    for k in range(KD):
                        mm = pe.matmul(pAB[o % 2][:, s, 0:TH], wff[:, k, o * P:(o + 1) * P],
                                       h[:, k, s * TH:(s + 1) * TH], start=(k == 0), stop=(k == KD - 1))
                mm.then_inc(f_mm, 1)

        @block.scalar
        def _(act):
            def squares(n):
                for k in range(KD):
                    act.wait_ge(ln_centre, n * KD + k + 1)
                    nc.scalar.activation((y if n else x_sq)[:, k, :], (h if n else xc)[:, k, :], ACT.Square)\
                        .then_inc(ln_sq, 1)

            squares(0)
            act.wait_ge(ln_var, 1)
            nc.scalar.activation(sq[:], sq[:], ACT.Sqrt).then_inc(ln_std, 1)
            act.wait_ge(ln_var, 2)
            nc.scalar.activation(ssum[:], ssum[:], ACT.Sqrt).then_inc(ln_std, 1)

            def split_hi(slot, tile, tiles_done=None):
                act.wait_ge(w_in[slot], tile)
                if tiles_done is not None:
                    act.wait_ge(proj_done, tiles_done)
                nc.scalar.copy(w_hi[slot][:], w_raw[slot][:]).then_inc(w_hi_done, 1)

            split_hi(0, 16)
            split_hi(1, 16)
            for k in range(KD):
                act.wait_ge(ln_out, k + 1)
                nc.scalar.copy(h_hi[:, k, :], xc[:, k, :]).then_inc(h_hi_done, 1)
            act.wait_ge(const_in, 16 * 10)
            nc.scalar.activation(hexp[:], hpar[:, 1:2], ACT.Exp).then_inc(dt_act, 1)
            act.wait_ge(proj_done, 1)
            nc.scalar.activation(flat(th), halves(pB), ACT.Abs, bias=hpar[:, 0:1]).then_inc(dt_abs, 1)
            act.wait_ge(dt_abs, 1)
            nc.scalar.activation(th[:], th[:], ACT.Exp, scale=-1.0).then_inc(dt_act, 1)
            act.wait_ge(dt_act, 2)
            nc.scalar.activation(th[:], th[:], ACT.Ln, bias=1.0).then_inc(dt_act, 1)
            act.wait_ge(cs_split, 3)
            nc.scalar.mul(cs_parts(1), cs_parts(0), -1.0).then_inc(cs_negd, 1)

            act.wait_ge(halved, 1)

            def group(g):
                def split(t):
                    split_hi(t % 2, g * (8 * TPG) + 16 * (t // 2 + 2), g * TPG + (t + 1))

                def conv_tap(c, buf, t):
                    act.wait_ge(proj_done, g * TPG + (t + 2))
                    if c >= 2:
                        act.wait_ge(yg_done, g * KG + (c - 1))
                    w = par[:, bass.ds(g * CPG + c, 1), :].squeeze(1)
                    nc.scalar.activation(flat(buf), halves(bank(t)), ACT.Identity, bias=w[:, CONV:CONV + 1],
                                         scale=w[:, CONV - 1:CONV]).then_inc(conv_done, 1)

                def conv_tanh(c, buf):
                    act.wait_ge(conv_done, g * (CST * CPG) + CST * (c + 1))
                    if c:
                        act.wait_ge(silu_done, g * CPG + c)
                    else:
                        act.wait_ge(out_added, g * KD + KD)
                    nc.scalar.activation(th[:], buf[:, :], ACT.Tanh).then_inc(tanh_c, 1)

                def gate_tanh(q):
                    act.wait_ge(proj_done, g * TPG + (5 + 2 * q))
                    if q:
                        act.wait_ge(sq_done, g * KG + q)
                        act.wait_ge(yl_done, g * KG + q)
                    nc.scalar.activation(flat(gate), halves(pB), ACT.Tanh, scale=0.5).then_inc(tanh_g, 1)

                def exps(q, n):
                    act.wait_ge(seg_mm, g * (4 * KG) + (4 * q + n + 2))
                    nc.scalar.activation(m_t[0:S, 2 * n:2 * n + 2].rearrange("p b h i -> p (b h i)"),
                                         pS[0:S, 0:4 * S], ACT.Exp).then_inc(exp_done, 1)

                def y_out(q):
                    act.wait_ge(yg_done, g * KG + (q + 2))
                    w = par[:, bass.ds(g * CPG + (2 + q), 1), :].squeeze(1)
                    nc.scalar.activation(y_hi[:, q, :], gate[:], ACT.Copy, scale=w[:, NPAR - 1:NPAR])\
                        .then_inc(y_done, 1)
                    if q >= 2:
                        act.wait_ge(sum_done, g * (KG - 1) + (q - 1))
                    nc.scalar.activation((sq if q else ssum)[:], gate[:], ACT.Square).then_inc(sq_done, 1)

                split(0)
                conv_tap(0, cB, 0)
                split(1)
                conv_tanh(0, cB)
                conv_tap(1, cC, 1)
                split(2)
                conv_tanh(1, cC)
                for q in range(KG):
                    if q:
                        split(2 + 2 * q)
                        gate_tanh(q - 1)
                        y_out(q - 1)
                    split(3 + 2 * q)
                    conv_tap(2 + q, hid, 2 + 2 * q)
                    exps(q, 0)
                    exps(q, 1)
                    conv_tanh(2 + q, hid)
                    exps(q, 2)
                    exps(q, 3)
                o0 = 2 + 2 * KG
                split(o0)
                gate_tanh(KG - 1)
                y_out(KG - 1)
                split(o0 + 1)
                act.wait_ge(gn_var, g + 1)
                nc.scalar.activation(small[:], small[:], ACT.Sqrt).then_inc(gn_std, 1)
                split(o0 + 2)
                act.wait_ge(gn_bc, g + 1)
                for s in range(2):
                    nc.scalar.copy(flat(rs)[:, s], [pT, pS][s][:, 0:TH]).then_inc(gn_rs, 1)
                for o in range(3, KD):
                    split(o0 + o)

            with act.Fori(0, G) as g:
                group(g)

            squares(1)
            act.wait_ge(ln_var, 3)
            nc.scalar.activation(ln_r[:], ln_r[:], ACT.Sqrt).then_inc(ln_std, 1)
            for b in range(NB):
                act.wait_ge(mx_done, b + 1)
                if b >= 2:
                    act.wait_ge(pt_mm, b - 1)
                nc.scalar.activation(prob[b % 2][:], [pT, pS][b % 2][0:S, 0:LK], ACT.Exp, bias=stat[:, 0, b:b + 1],
                                     accum_out=stat[:, 1, b:b + 1]).then_inc(ex_done, 1)
            act.wait_ge(ffn_in, 16 * 5)
            for k in range(KD):
                nc.scalar.activation(wff[:, k, :], wff[:, k, :], ACT.Sign).then_inc(sign_done, 1)
            squares(2)
            act.wait_ge(ln_var, 4)
            nc.scalar.activation(ln_r[:], ln_r[:], ACT.Sqrt).then_inc(ln_std, 1)
            act.wait_ge(r_own, 1)
            nc.scalar.activation(route[:], route[:], ACT.Exp).then_inc(r_exp, 1)
            for o in range(KD):
                act.wait_ge(os_mm, o + 1)
                if o >= 2:
                    act.wait_ge(f_done, 2 * (o - 1))
                nc.scalar.copy(flat(oscale[o % 2]), halves(pY)).then_inc(os_copy, 1)

        @block.gpsimd
        def _(pool):
            nc.gpsimd.memset(ones[:], 1.0).then_inc(ones_set, 1)
            for k in range(KD):
                pool.wait_ge(ln_tmp, k + 1)
                nc.gpsimd.tensor_tensor(acc[:, k, :], acc[:, k, :], [gate, hid][k % 2][:], ALU.add)\
                    .then_inc(acc_ln, 1)

            def group(g):
                for q in range(1, KG):
                    pool.wait_ge(sq_done, g * KG + (q + 1))
                    if q >= 2:
                        pool.wait_ge(sum_done, g * (KG - 1) + (q - 1))
                    nc.gpsimd.tensor_tensor(ssum[:], ssum[:], sq[:], ALU.add).then_inc(sum_done, 1)
                for o in range(KD):
                    pool.wait_ge(out_scaled, g * KD + (KD + o + 1))
                    nc.gpsimd.tensor_tensor(acc[:, o, :], acc[:, o, :], tmp[o % 2][:], ALU.add).then_inc(out_added, 1)

            with pool.Fori(0, G) as g:
                group(g)

        @block.vector
        def _(v):
            stt = nc.vector.scalar_tensor_tensor
            tt = nc.vector.tensor_tensor
            ts = nc.vector.tensor_scalar

            def centre(n):
                v.wait_ge(ln_sum, 2 * n + 1)
                for k in range(KD):
                    stt(flat3(h if n else xc, k), halves(pY), -1.0 / D, flat3(acc, k), ALU.mult, ALU.add).then_inc(ln_centre, 1)

            def split_lo(slot, tiles):
                v.wait_ge(w_hi_done, tiles)
                tt(w_lo[slot][:], w_raw[slot][:], w_hi[slot][:].bitcast(F32), ALU.subtract).then_inc(w_lo_done, 1)

            def flat3(buf, k):
                return buf[:, k, :].rearrange("p (s n) -> p s n", s=2)

            v.sem_inc(out_scaled, KD)
            v.sem_inc(out_added, KD)
            v.sem_inc(skip_done, 1)
            v.sem_inc(exp_done, 1)
            v.sem_inc(hc_done, 1)
            v.sem_inc(yg_done, 1)
            v.sem_inc(seg_mm, 1)
            centre(0)
            v.wait_ge(ln_sum, 2)
            ts(flat(sq), halves(pA), 1.0 / D, EPS, ALU.mult, ALU.add).then_inc(ln_var, 1)
            v.wait_ge(ln_std, 1)
            nc.vector.reciprocal(th[:], sq[:]).then_inc(ln_own, 1)
            v.wait_ge(ln_own, 1)
            tt(hid[:], th[:], th[:], ALU.mult).then_inc(ln_own, 1)
            v.wait_ge(ln_own, 2)
            stt(flat(ssum), halves(pA), 1.0 / D, flat(hid), ALU.mult, ALU.mult).then_inc(ln_own, 1)
            v.wait_ge(ln_own, 3)
            ts(ssum[:], ssum[:], EPS, None, ALU.add).then_inc(ln_var, 1)
            v.wait_ge(ln_std, 2)
            nc.vector.reciprocal(sq[:], ssum[:]).then_inc(ln_own, 1)
            v.wait_ge(ln_own, 4)
            tt(ssum[:], sq[:], th[:], ALU.mult).then_inc(ln_own, 1)
            v.wait_ge(ln_own, 5)
            v.wait_ge(const_in, 16 * 10)
            for i in range(2):
                split_lo(i, i + 1)

            def h_split(k):
                v.wait_ge(h_hi_done, k + 1)
                tt(h_lo[:, k, :], xc[:, k, :], h_hi[:, k, :].bitcast(F32), ALU.subtract).then_inc(h_lo_done, 1)
            for k in range(KD):
                if k >= 2:
                    v.wait_ge(acc_ln, k - 1)
                tt([gate, hid][k % 2][:], xc[:, k, :], th[:], ALU.mult).then_inc(ln_tmp, 1)
                v.wait_ge(ln_tmp, k + 1)
                stt(xc[:, k, :], xc[:, k, :], nw[:, k:k + 1], ssum[:], ALU.mult, ALU.mult).then_inc(ln_out, 1)
                if k:
                    h_split(k - 1)
            h_split(KD - 1)
            ts(par[:, :, 0:CONV + 1], par[:, :, 0:CONV + 1], 0.5, None, ALU.mult).then_inc(dt_own, 1)
            ts(par[:, :, NPAR - 1:NPAR], par[:, :, NPAR - 1:NPAR], 0.5, None, ALU.mult).then_inc(halved, 1)

            v.wait_ge(proj_done, 1)
            v.wait_ge(acc_ln, KD)
            v.wait_ge(dt_abs, 1)
            ts(flat(gate), halves(pB), hpar[:, 0:1], 0.0, ALU.add, ALU.max).then_inc(dt_max, 1)
            v.wait_ge(dt_act, 3)
            v.wait_ge(dt_max, 1)
            tt(gate[:], gate[:], th[:], ALU.add).then_inc(dt_own, 1)
            v.wait_ge(dt_own, 2)
            ts(hid[:], gate[:], hexp[:, 0:1], -1.0, ALU.mult, ALU.mult).then_inc(dt_own, 1)
            for n in range(4):
                v.wait_ge(dt_tr, n + 1)
                src = [pT, pS][n % 2][0:S, :]
                dst = dt_tok[:].rearrange("p b h -> p (b h)") if n < 2 else m_flat[0:S]
                nc.vector.tensor_copy(dst[:, n % 2 * HB * P:(n % 2 + 1) * HB * P], src).then_inc(dt_copy, 1)
            v.wait_ge(cs_mm, 1)
            parts = [cs_parts(0)[:, c * T:(c + 1) * T] for c in range(3)]
            nc.vector.tensor_copy(flat(sq), halves(pY)).then_inc(dt_own, 1)
            v.wait_ge(dt_own, 4)
            nc.vector.tensor_copy(parts[0], sq[:]).then_inc(cs_split, 1)
            v.wait_ge(cs_split, 1)
            tt(sq[:], sq[:], parts[0], ALU.subtract).then_inc(dt_own, 1)
            v.wait_ge(dt_own, 5)
            nc.vector.tensor_copy(parts[1], sq[:]).then_inc(cs_split, 1)
            v.wait_ge(cs_split, 2)
            tt(sq[:], sq[:], parts[1], ALU.subtract).then_inc(dt_own, 1)
            v.wait_ge(dt_own, 6)
            nc.vector.tensor_copy(parts[2], sq[:]).then_inc(cs_split, 1)
            v.wait_ge(cs_negd, 1)
            v.wait_ge(halved, 1)

            def group(g):
                def split(t):
                    split_lo(t % 2, g * TPG + (t + 3))

                def taps(c, buf, t):
                    w = par[:, bass.ds(g * CPG + c, 1), :].squeeze(1)
                    for n in range(1, CONV):
                        for s in range(2):
                            v.wait_ge(conv_done, g * (CST * CPG) + (CST * c + (1 if n == 1 else 2 * n - 2 + s)))
                            stt(shifted(buf, n)[:, s], batches(bank(t))[:, s, :, 0:S - n],
                                w[:, CONV - 1 - n:CONV - n], shifted(buf, n)[:, s], ALU.mult, ALU.add)\
                                .then_inc(conv_done, 1)

                def silu(c, buf):
                    v.wait_ge(tanh_c, g * CPG + (c + 1))
                    stt(buf[:, :], th[:], 1.0, buf[:, :], ALU.add, ALU.mult).then_inc(silu_done, 1)

                def cb_out(s):
                    v.wait_ge(cb_mm, g * 2 + (s + 1))
                    nc.vector.tensor_copy(g_t[:, s * HB:(s + 1) * HB, :].rearrange("p b i -> p (b i)"),
                                          pT[0:S, 0:TH]).then_inc(cb_copy, 1)

                def gate_out(q):
                    v.wait_ge(tanh_g, g * KG + (q + 1))
                    stt(flat(gate), flat(gate), 1.0, halves(pB), ALU.add, ALU.mult).then_inc(gated, 1)

                def tokens_out(q, s):
                    if q == 0 and s == 0:
                        v.wait_ge(dt_in, g * 16 + 16)
                    v.wait_ge(tr_done, g * (2 * KG) + (2 * q + s + 1))
                    bs = slice(s * HB, (s + 1) * HB)
                    tt(hc[:, bs, :].rearrange("p b (h c) -> p b h c", h=2),
                       pT[0:S, :].rearrange("p (b h c) -> p b h c", b=HB, h=2),
                       bc(dt_g[:, bs, 2 * q:2 * q + 2].unsqueeze(3), [S, HB, 2, HP]),
                       ALU.mult).then_inc(hc_done, 1)

                def decay(q, s):
                    if q == 0 and s == 0:
                        v.wait_ge(cb_copy, g * 2 + 2)
                    v.wait_ge(exp_done, g * (4 * KG) + (4 * q + 2 * s + 3))
                    bs = slice(s * HB, (s + 1) * HB)
                    tt(m_t[0:S, bs], m_t[0:S, bs], bc(g_t[:, bs, :].unsqueeze(2), [S, HB, 2, S]),
                       ALU.mult).then_inc(m_done, 1)

                def skip(q):
                    v.wait_ge(y_mm, g * (2 * KG) + (2 * q + 2))
                    w = par[:, bass.ds(g * CPG + (2 + q), 1), :].squeeze(1)
                    stt(flat(hid), flat(hid), w[:, CONV + 1:CONV + 2], halves(pY), ALU.mult, ALU.add)\
                        .then_inc(skip_done, 1)

                def gate_y(q):
                    v.wait_ge(skip_done, g * KG + (q + 2))
                    tt(gate[:], gate[:], hid[:], ALU.mult).then_inc(yg_done, 1)

                def y_low(q):
                    v.wait_ge(y_done, g * KG + (q + 1))
                    w = par[:, bass.ds(g * CPG + (2 + q), 1), :].squeeze(1)
                    stt(y_lo[:, q, :], gate[:], w[:, NPAR - 1:NPAR], y_hi[:, q, :].bitcast(F32), ALU.mult,
                        ALU.subtract).then_inc(yl_done, 1)

                def y_steps(q):
                    gate_out(q)
                    tokens_out(q, 0)
                    decay(q, 0)
                    tokens_out(q, 1)
                    decay(q, 1)
                    skip(q)
                    gate_y(q)

                split(0)
                taps(0, cB, 0)
                split(1)
                silu(0, cB)
                taps(1, cC, 1)
                split(2)
                silu(1, cC)
                for q in range(KG):
                    if q:
                        split(2 + 2 * q)
                        y_steps(q - 1)
                        y_low(q - 1)
                    split(3 + 2 * q)
                    taps(2 + q, hid, 2 + 2 * q)
                    if q == 0:
                        cb_out(0)
                        cb_out(1)
                    silu(2 + q, hid)
                o0 = 2 + 2 * KG
                split(o0)
                y_steps(KG - 1)
                y_low(KG - 1)
                split(o0 + 1)
                v.wait_ge(gn_mm, g + 1)
                ts(small[:], pS[0:S, 0:NB], 0.25 / (DI // G), EPS, ALU.mult, ALU.add).then_inc(gn_var, 1)
                v.wait_ge(gn_std, g + 1)
                nc.vector.reciprocal(small[:], small[:]).then_inc(gn_r, 1)
                v.wait_ge(gn_r, g + 1)
                for s in range(2):
                    tt(diag[0:S, s * TH:(s + 1) * TH].rearrange("p (b i) -> p b i", b=HB),
                       bc(ident[0:S, 0:S].unsqueeze(1), [S, HB, S]),
                       bc(small[:, s * HB:(s + 1) * HB].unsqueeze(2), [S, HB, S]), ALU.mult).then_inc(gn_diag, 1)
                split(o0 + 2)
                v.wait_ge(gn_rs, g * 2 + 2)
                for o in range(KD):
                    t = o0 + o
                    if o >= 2:
                        split(t + 1) if t + 1 < TPG else None
                    v.wait_ge(proj_done, g * TPG + (t + 2))
                    if o >= 2:
                        v.wait_ge(out_added, g * KD + (KD + o - 1))
                    else:
                        v.wait_ge(sum_done, g * (KG - 1) + (KG - 1))
                    tt(flat(tmp[o % 2]), halves(bank(t)), flat(rs), ALU.mult).then_inc(out_scaled, 1)

            with v.Fori(0, G) as g:
                group(g)

            def layer_norm(n):
                centre(n)
                v.wait_ge(ln_sum, 2 * n + 2)
                ts(flat(ln_r), halves(pA), 1.0 / D, EPS, ALU.mult, ALU.add).then_inc(ln_var, 1)
                v.wait_ge(ln_std, 2 + n)
                nc.vector.reciprocal(oscale[0][:], ln_r[:]).then_inc(ln_own, 1)
                v.wait_ge(ln_own, 5 + n)
                for k in range(KD):
                    tt(h[:, k, :], h[:, k, :], oscale[0][:], ALU.mult).then_inc(ln_out, 1)

            layer_norm(1)
            for b in range(NB + 1):
                if b < NB:
                    ps = [pT, pS][b % 2]
                    v.wait_ge(sc_mm, b + 1)
                    nc.vector.tensor_reduce(stat[:, 3, b:b + 1], ps[0:S, 0:LK], AX.X, ALU.max).then_inc(sub_done, 1)
                    v.wait_ge(sub_done, 2 * b + 1)
                    ts(stat[:, 0, b:b + 1], stat[:, 3, b:b + 1], -1.0, None, ALU.mult).then_inc(mx_done, 1)
                    v.wait_ge(ex_done, b + 1)
                    nc.vector.reciprocal(stat[:, 2, b:b + 1], stat[:, 1, b:b + 1]).then_inc(sub_done, 1)
                    v.wait_ge(sub_done, 2 * b + 2)
                    ts(prob[b % 2][:], prob[b % 2][:], stat[:, 2, b:b + 1], None, ALU.mult).then_inc(pn_done, 1)
                    v.wait_ge(pt_mm, b + 1)
                    nc.vector.tensor_copy(prob_t[b % 2][:].rearrange("p c i -> p (c i)"), pA[0:LC, b % 2, 0:CK * S])\
                        .then_inc(pt_copy, 1)
                if b:
                    c = b - 1
                    v.wait_ge(xo_mm, c + 1)
                    xa = acc[:, :, c * S:(c + 1) * S].rearrange("p (s d) i -> p s d i", s=2)
                    tt(xa, batches([pY, pB][c % 2]), xa, ALU.add).then_inc(x2_done, 1)

            v.wait_ge(x2_done, NB)
            layer_norm(2)
            v.wait_ge(r_mm, 1)
            logits = pT[0:S, 0:NB * NE].rearrange("p (b e) -> p b e", b=NB)
            nc.vector.tensor_reduce(rstat[:, 0, :], logits, AX.X, ALU.max).then_inc(sub_done, 1)
            v.wait_ge(sub_done, 2 * NB + 1)
            tt(route[:], logits, bc(rstat[:, 0, :].unsqueeze(2), [S, NB, NE]), ALU.subtract).then_inc(r_own, 1)
            v.wait_ge(r_exp, 1)
            nc.vector.tensor_reduce(rstat[:, 1, :], route[:], AX.X, ALU.add).then_inc(r_own, 1)
            v.wait_ge(r_own, 2)
            nc.vector.reciprocal(rstat[:, 0, :], rstat[:, 1, :]).then_inc(r_own, 1)
            v.wait_ge(r_own, 3)
            tt(route[:], route[:], bc(rstat[:, 0, :].unsqueeze(2), [S, NB, NE]), ALU.mult).then_inc(r_own, 1)
            v.wait_ge(r_tr, 1)
            nc.vector.tensor_copy(route_t[:, 0:TH], pT[0:NE, 0:TH]).then_inc(sub_done, 1)
            nc.vector.tensor_copy(route_t[:, TH:T], pS[0:NE, 0:TH]).then_inc(r_copy, 1)
            for k in range(KD):
                v.wait_ge(is_mm, k + 1)
                tt(flat3(h, k), flat3(h, k), halves(pAB[k % 2]), ALU.mult).then_inc(xs_done, 1)
            for o in range(KD):
                v.wait_ge(f_mm, o + 1)
                v.wait_ge(os_copy, o + 1)
                tt(flat(oscale[o % 2]), halves(pAB[o % 2]), flat(oscale[o % 2]), ALU.mult).then_inc(f_scaled, 1)
                v.wait_ge(f_scaled, o + 1)
                for s in range(2):
                    cols = slice(s * TH, (s + 1) * TH)
                    stt(acc[:, o, cols], oscale[o % 2][:, cols], fb[:, o:o + 1], acc[:, o, cols], ALU.add, ALU.add)\
                        .then_inc(f_done, 1)


def kernel(**inputs):
    import ml_dtypes
    import concourse.bacc as bacc
    from concourse.bass_utils import run_bass_kernel_spmd as run

    A = {k: np.asarray(v) for k, v in inputs.items()}
    L = "L0_attn_"

    def channels(v):
        return np.moveaxis(v.reshape(-1, P, *v.shape[1:]), 1, 0)

    w_in = A[L + "in_proj_w"].reshape(-1, P, KD, P).transpose(0, 3, 2, 1)
    w_out = A[L + "out_proj_w"].reshape(KD, P, G, KG, P).transpose(2, 0, 4, 3, 1)
    n_di = DI // P
    order = []
    for g in range(G):
        tiles = [w_in[2 * n_di + g], w_in[2 * n_di + G + g]]
        for q in range(KG):
            tiles += [w_in[n_di + g * KG + q], w_in[g * KG + q]]
        order += tiles + [w_out[g, o] for o in range(KD)]
    conv_w, conv_b = A[L + "conv_w"], A[L + "conv_b"]
    skip = np.repeat(A[L + "Dp"], HP)
    par_c = np.zeros((conv_w.shape[0], NPAR), np.float32)
    par_c[:, 0:CONV], par_c[:, CONV] = conv_w, conv_b
    par_c[:DI, CONV + 1], par_c[:DI, CONV + 2] = skip, A[L + "gnorm_w"]
    par_t = par_c.reshape(-1, P, NPAR)
    par = np.stack([par_t[t] for g in range(G) for t in [n_di + g, n_di + G + g] + list(range(g * KG, (g + 1) * KG))], 1)

    const32 = np.zeros((P, P + S), np.float32)
    const32[:, :P] = np.eye(P)
    const32[:S, P:] = np.triu(np.ones((S, S)))
    bf = ml_dtypes.bfloat16
    mask = np.zeros((S, 5, S), np.float32)
    mask[:, 0:4] = np.where(np.arange(S)[None, :] < np.arange(S)[:, None], MASKED, 0.0)[:, None, :]
    mask[:, 4] = np.eye(S)
    seg_r0 = np.zeros((SEGK, HB, 2, S), np.float32)
    seg_r0[3:6, :, 0], seg_r0[6:9, :, 1] = 1, 1
    seg_l0 = np.zeros((SEGK, HB, S), np.float32)
    seg_l0[0:3] = 1

    arrays = {
        "x_t": A["x"].reshape(T, D).T,
        "w_main": np.stack([w_in[-1]] + order + order[:1]),
        "par": par,
        "norm_w": channels(A[L + "norm_w"]),
        "head_par": np.stack([A[L + "dt_bias"], A[L + "A_log"]], 1),
        "const32": const32,
        "mask": mask.astype(bf),
        "seg_r0": seg_r0.astype(bf),
        "seg_l0": seg_l0.astype(bf),
        "ctx_t": A["ctx_4096"].transpose(0, 2, 1),
        "ctx_n": A["ctx_4096"],
        "w_ffn": A["L0_ffn_weight"].reshape(D, KD, P).transpose(2, 1, 0),
        "gate_w": A["L0_ffn_gate_w"].T,
        "in_scale": A["L0_ffn_in_channel_scale"],
        "out_scale": A["L0_ffn_out_channel_scale"],
        "ffn_bias": channels(A["L0_ffn_bias"]),
    }
    arrays = {k: np.ascontiguousarray(v) for k, v in arrays.items()}
    nc = bacc.Bacc("TRN2", target_bir_lowering=False, num_devices=1)
    arrays = {f"in_{k}": v for k, v in arrays.items()}
    args = [nc.dram_tensor(k, v.shape, mybir.dt.from_np(v.dtype), kind="ExternalInput").ap() for k, v in arrays.items()]
    out = nc.dram_tensor("out_t", (D, T), F32, kind="ExternalOutput").ap()
    build(nc, *args, out)
    r = run(nc, [arrays], core_ids=[0])
    return np.ascontiguousarray(r.results[0]["out_t"].T).reshape(NB, S, D)
```

```python
from contextlib import ExitStack

import numpy as np

import concourse.bass as bass
from concourse import mybir

F32 = mybir.dt.float32
BF16 = mybir.dt.bfloat16
F32R = mybir.dt.float32r
ALU = mybir.AluOpType
ACT = mybir.ActivationFunctionType
AX = mybir.AxisListType

P = 128
NB, S, D = 8, 112, 1024
T = NB * S
TH = T // 2
HB = NB // 2
KD = D // P
HEADS, HP, G = 128, 64, 8
DI = HEADS * HP
KG = DI // G // P
TPG = 2 + 2 * KG + KD
CONV = 4
CST = 1 + 2 * (CONV - 1)
CPG = 2 + KG
NPAR = CONV + 3
EPS = 1e-5
LK, CK = 375, 3
LC = LK // CK
NE = 8
NE3 = 3 * NE
MASKED = -1e30
CSK = 9
SEGK = CSK + S


def bc(ap, shape):
    return ap.broadcast_to(shape)


def build(nc, x_t, w_main, par_d, norm_w, head_par, const32, seg_r0, seg_l0, ctx_t, ctx_n,
          w_ffn, gate_w, scales, lo_rows, ffn_bias, out):
    with ExitStack() as ctx:
        def sb(name, shape, dt=F32, scope=ctx):
            return scope.enter_context(nc.sbuf_tensor(name, shape, dt))

        def sem(name):
            return ctx.enter_context(nc.semaphore(name))

        pA = ctx.enter_context(nc.psum_tensor("pA", [P, 2, 512], F32))
        pB = ctx.enter_context(nc.psum_tensor("pB", [P, 2, 512], F32))
        pY = ctx.enter_context(nc.psum_tensor("pY", [P, 2, 512], F32))
        pT = ctx.enter_context(nc.psum_tensor("pT", [P, 512], F32))
        pS = ctx.enter_context(nc.psum_tensor("pS", [P, 512], F32))
        pAB = [pA, pB]

        def halves(ps):
            return ps[:, :, 0:TH]

        def batches(ps):
            return ps[:, :, 0:TH].rearrange("p s (b i) -> p s b i", b=HB)

        acc = sb("acc", [P, KD, T])
        ident = sb("ident", [P, P])
        ones = sb("ones", [P, P])

        mixer = ExitStack()
        h_hi = sb("h_hi", [P, KD, T], F32R, scope=mixer)
        h_lo = sb("h_lo", [P, KD, T], F32R, scope=mixer)
        w_raw = [sb(f"w_raw{i}", [P, KD, P], scope=mixer) for i in range(2)]
        w_hi = [sb(f"w_hi{i}", [P, KD, P], F32R, scope=mixer) for i in range(2)]
        w_lo = [sb(f"w_lo{i}", [P, KD, P], F32R, scope=mixer) for i in range(2)]
        start = ExitStack()
        xc = sb("xc", [P, KD, T], scope=start)
        x_sq = sb("x_sq", [P, KD, T], scope=start)
        start.close()
        y_hi = sb("y_hi", [P, KG, T], F32R, scope=mixer)
        y_lo = sb("y_lo", [P, KG, T], F32R, scope=mixer)
        par = sb("par", [P, G * CPG, NPAR], scope=mixer)
        nw = sb("nw", [P, KD], scope=mixer)
        hpar = sb("hpar", [P, 2], scope=mixer)
        hexp = sb("hexp", [P, 1], scope=mixer)
        tri = sb("tri", [S, S], scope=mixer)
        seg_r = [sb(f"seg_r{i}", [SEGK, HB, 2, S], BF16, scope=mixer) for i in range(2)]
        seg_l = [sb(f"seg_l{i}", [SEGK, HB, S], BF16, scope=mixer) for i in range(2)]
        dt_g = sb("dt_g", [S, NB, 2 * KG], scope=mixer)
        hid = sb("hid", [P, T], scope=mixer)
        gate = sb("gate", [P, T], scope=mixer)
        th = sb("th", [P, T], scope=mixer)
        hc = sb("hc", [S, NB, P], scope=mixer)
        m_t = sb("m_t", [P, NB, 2, S], scope=mixer)
        g_t = sb("g_t", [S, NB, S], scope=mixer)
        sq = sb("sq", [P, T], scope=mixer)
        ssum = sb("ssum", [P, T], scope=mixer)
        x_small = sb("x_small", [S, 7, NB], scope=mixer)
        small = sb("small", [S, NB], scope=mixer)
        tmp = [sq, th]
        diag, rs = hid, gate
        m_flat = m_t[:].rearrange("p b h i -> p (b h i)")
        cB, cC = m_flat[:, 0:T], m_flat[:, T:2 * T]
        mixer.close()

        tail = ExitStack()
        scale3 = sb("scale3", [NE3, 2, D], F32R, scope=tail)
        early = ExitStack()
        ctxt_sb = [sb(f"ctxt_sb{i}", [P, KD, LK], scope=early) for i in range(2)]
        ctxn_sb = [sb(f"ctxn_sb{i}", [LC, CK, D], scope=early) for i in range(2)]
        early.close()
        xs_lo = sb("xs_lo", [P, KD, T], F32R, scope=tail)
        route3 = sb("route3", [S, 2, NB, NE3], F32R, scope=tail)
        route = sb("route", [S, 2, NB, NE], scope=tail)
        route_t = sb("route_t", [NE3, 2, T], F32R, scope=tail)
        oscale = [sb(f"oscale{i}", [P, T], scope=tail) for i in range(3)]
        h = sb("h", [P, KD, T], scope=tail)
        late = ExitStack()
        y = sb("y", [P, KD, T], scope=late)
        late.close()
        xs_hi = sb("xs_hi", [P, KD, T], F32R, scope=tail)
        y_flat = y[:].rearrange("p k t -> p (k t)")
        ctx_cols = [ctxt_sb[0][:], ctxt_sb[1][:], y_flat[:, 0:KD * LK].rearrange("p (k n) -> p k n", k=KD)]
        ctx_rows = [ctxn_sb[0][:], ctxn_sb[1][:],
                    y_flat[0:LC, KD * LK:KD * LK + CK * D].rearrange("p (c d) -> p c d", c=CK)]
        late = ExitStack()
        wff_raw = sb("wff_raw", [P, KD, D], scope=late)
        late.close()
        wff = sb("wff", [P, KD, D], F32R, scope=tail)
        sq2 = [sb(f"sq2_{i}", [P, KD, S], scope=tail) for i in range(2)]
        pre_1 = sq2[0]
        pre = sb("pre", [P, 2, S], scope=tail)
        pre_sq = sb("pre_sq", [P, 2, S], scope=tail)
        prob = [sb(f"prob{i}", [S, LK], scope=tail) for i in range(2)]
        prob_t = [sb(f"prob_t{i}", [LC, CK, S], scope=tail) for i in range(2)]
        stat = sb("stat", [S, 6, NB], scope=tail)
        gw = sb("gw", [P, KD, NE], scope=tail)
        fb = sb("fb", [P, KD], scope=tail)
        lo_row = sb("lo_row", [NE3, 1], scope=tail)
        rstat = sb("rstat", [S, 5, NB], scope=tail)
        wff_flat = wff_raw[:].rearrange("p k d -> p (k d)")
        scale_raw, scale_tmp = wff_flat[0:NE3, 0:2 * D], wff_flat[0:NE3, 2 * D:4 * D]
        tail.close()

        cs_pos = nc.dram_tensor("cs_pos", (HEADS, 3, T), BF16).ap()
        cs_neg = nc.dram_tensor("cs_neg", (HEADS, 3, T), BF16).ap()
        dt_dram = nc.dram_tensor("dt_dram", (G, S, NB, 2 * KG), F32).ap()

        x_in = [sem(f"x_in{i}") for i in range(4)]
        const_in = sem("const_in")
        w_in = [sem(f"w_in{i}") for i in range(2)]
        w_hi_done, w_lo_done = sem("w_hi_done"), sem("w_lo_done")
        h_hi_done = sem("h_hi_done")
        h_lo_done = [sem("h_lo_even"), sem("h_lo_odd")]
        dt_in, yl_done = sem("dt_in"), sem("yl_done")
        seg_in = [sem(f"seg_in{i}") for i in range(2)]
        cs_out = sem("cs_out")
        x_mean, x_centred, x_squared, x_summed, x_sq_mm, x_stat, x_std = (
            sem(x) for x in ("x_mean", "x_centred", "x_squared", "x_summed", "x_sq_mm", "x_stat", "x_std"))
        x_diag, x_bc, std_copy, x_tmp, acc_ln, ln_out = (
            sem(x) for x in ("x_diag", "x_bc", "std_copy", "x_tmp", "acc_ln", "ln_out"))
        ones_set = sem("ones_set")
        dt_abs, dt_max, dt_act, dt_own, dt_tr, dt_copy, cs_mm, cs_split, cs_negd = (
            sem(x) for x in ("dt_abs", "dt_max", "dt_act", "dt_own", "dt_tr", "dt_copy", "cs_mm", "cs_split", "cs_negd"))
        halved = sem("halved")
        proj_done = sem("proj_done")
        conv_done = sem("conv_done")
        tanh_c, silu_done = sem("tanh_c"), sem("silu_done")
        tanh_g, gated = sem("tanh_g"), sem("gated")
        seg_mm, exp_done = sem("seg_mm"), sem("exp_done")
        cb_mm, cb_copy = sem("cb_mm"), sem("cb_copy")
        tr_done, hc_done = sem("tr_done"), sem("hc_done")
        m_done = sem("m_done")
        y_mm, skip_done, yg_done, y_done, sq_done, sum_done = (
            sem(x) for x in ("y_mm", "skip_done", "yg_done", "y_done", "sq_done", "sum_done"))
        gn_mm, gn_var, gn_std, gn_r, gn_diag, gn_bc, gn_rs = (
            sem(x) for x in ("gn_mm", "gn_var", "gn_std", "gn_r", "gn_diag", "gn_bc", "gn_rs"))
        out_scaled, out_added = sem("out_scaled"), sem("out_added")
        ctx_in = [sem(f"ctx_in{i}") for i in range(3)]
        scale_in, ffn_in, wff_in = sem("scale_in"), sem("ffn_in"), sem("wff_in")
        scale_hi, scale_x, scale_done = sem("scale_hi"), sem("scale_x"), sem("scale_done")
        mean_mm, centred, squared, squares_summed, sq_mm, var_done, std_done, inv_std = (
            sem(x) for x in ("mean_mm", "centred", "squared", "squares_summed", "sq_mm", "var_done", "std_done", "inv_std"))
        sc_mm, mx_raw, mx_done, ex_done, ri_done, pn_done, pt_mm, pt_copy, xo_mm, x2_done = (
            sem(x) for x in ("sc_mm", "mx_raw", "mx_done", "ex_done", "ri_done", "pn_done", "pt_mm", "pt_copy",
                             "xo_mm", "x2_done"))
        pre_done, mean2_mm, centred2, squared2, pre_sq_done, sq2_mm = (
            sem(x) for x in ("pre_done", "mean2_mm", "centred2", "squared2", "pre_sq_done", "sq2_mm"))
        sign_done = sem("sign_done")
        r_own, r_std, r_exp, r_hi, r_lo, r_tr, r_copy, r_turned = (
            sem(x) for x in ("r_own", "r_std", "r_exp", "r_hi", "r_lo", "r_tr", "r_copy", "r_turned"))
        is_mm, xs_done, xs_hi_done, xs_lo_done = (sem(x) for x in ("is_mm", "xs_done", "xs_hi_done", "xs_lo_done"))
        f_mm, os_mm, os_copy, f_scaled, f_done, stored = (
            sem(x) for x in ("f_mm", "os_mm", "os_copy", "f_scaled", "f_done", "stored"))

        dt_tok = hc

        def bank(t):
            o = t - (2 + 2 * KG)
            return [pA, pB, pY][o % 3] if o >= 0 else [pA, pB][t % 2]

        ALL_OUT = G * KD

        block = ctx.enter_context(nc.Block())

        def da_t(b):
            return m_flat[0:S, b * HEADS:(b + 1) * HEADS]

        def cs_parts(i):
            return x_sq[:].rearrange("p k t -> p (k t)").bitcast(BF16)[:, i * 3 * T:(i + 1) * 3 * T]

        def flat(buf):
            return buf[:, :].rearrange("p (s n) -> p s n", s=2)

        def shifted(buf, n):
            return buf[:, :].rearrange("p (s b i) -> p s b i", s=2, b=HB)[:, :, :, n:S]

        pre_x = sq[:].rearrange("p (b i) -> p b i", b=NB)

        def cols(b):
            return slice(b * S, (b + 1) * S)

        mean2 = pA[:, 0, 0:S]
        logits = pA[0:S, 1, 0:NB * NE].rearrange("p (b e) -> p b e", b=NB)
        sums_sq = pA[0:S, 1, NB * NE:(NE + 2) * NB].rearrange("p (n b) -> p n b", n=2)

        def f_bank(o, s):
            return [pY[:, s], [pT, pS][s][:], pB[:, s]][o % 3][:, 0:TH]

        @block.sync
        def _(sp):
            for i in range(4):
                k = slice(i * KD // 4, (i + 1) * KD // 4)
                sp.dma_start(acc[:, k, :], x_t.rearrange("(k p) t -> p k t", p=P)[:, k, :]).then_inc(x_in[i], 16)
            sp.dma_start(ident[:], const32[:, 0:P]).then_inc(const_in, 16)
            sp.dma_start(tri[:], const32[0:S, P:P + S]).then_inc(const_in, 16)
            sp.dma_start(nw[:], norm_w).then_inc(const_in, 16)
            sp.dma_start(hpar[:], head_par).then_inc(const_in, 16)
            sp.dma_start(par[:], par_d).then_inc(const_in, 16)

            def load_w(n, slot):
                sp.dma_start(w_raw[slot][:], w_main[n]).then_inc(w_in[slot], 16)

            load_w(0, 0)
            load_w(1, 1)
            for i in range(2):
                sp.dma_start(seg_r[i][:], seg_r0).then_inc(const_in, 16)
                sp.dma_start(seg_l[i][:], seg_l0).then_inc(const_in, 16)
            sp.wait_ge(w_lo_done, 1)
            load_w(2, 0)
            sp.wait_ge(dt_copy, 2)
            for g in range(G):
                sp.dma_start(dt_dram[g], dt_tok[:, :, g * 2 * KG:(g + 1) * 2 * KG]).then_inc(cs_out, 16)
            sp.wait_ge(cs_split, 3)
            sp.dma_start(cs_pos.rearrange("h c t -> h (c t)"), cs_parts(0)).then_inc(cs_out, 16)
            sp.wait_ge(cs_negd, 1)
            sp.dma_start(cs_neg.rearrange("h c t -> h (c t)"), cs_parts(1)).then_inc(cs_out, 16)
            sp.wait_ge(cs_out, 16 * (G + 2))
            sp.wait_ge(const_in, 16 * 9)

            def load_seg(g, q):
                sp.wait_ge(seg_mm, g * (4 * KG) + (4 * q + 1))
                heads = bass.ds(g * (2 * KG) + 2 * q, 2)
                pos = cs_pos[heads].rearrange("h c (s b i) -> c s b h i", s=2, b=HB)
                neg = cs_neg[heads].rearrange("h c (s b i) -> (h c) s b i", s=2, b=HB)
                for s in range(2):
                    for hh in range(2):
                        sp.dma_start(seg_r[s][0:3, :, hh, :], pos[:, s, :, hh, :]).then_inc(seg_in[s], 16)
                    sp.dma_start(seg_l[s][3:CSK], neg[:, s]).then_inc(seg_in[s], 16)

            def load_ctx(b):
                sp.dma_start(ctx_cols[b % 3], ctx_t[b].rearrange("(k p) n -> p k n", p=P)).then_inc(ctx_in[b % 3], 16)
                sp.dma_start(ctx_rows[b % 3], ctx_n[b].rearrange("(k p) n -> p k n", p=LC)).then_inc(ctx_in[b % 3], 16)

            def group(g, last):
                for j in range(TPG):
                    if not (last and j == TPG - 1):
                        sp.wait_ge(w_lo_done, g * TPG + (j + 2))
                        sp.dma_start(w_raw[(j + 1) % 2][:], w_main[bass.ds(g * TPG + (j + 3), 1)].squeeze(0))\
                            .then_inc(w_in[(j + 1) % 2], 16)
                    if j == 0:
                        sp.wait_ge(hc_done, g * (2 * KG) + 1)
                        sp.dma_start(dt_g[:], dt_dram[bass.ds(g, 1)].squeeze(0)).then_inc(dt_in, 16)
                        load_seg(g, 0)
                    if j >= 5 and j % 2 == 1 and j < 3 + 2 * KG:
                        load_seg(g, (j - 3) // 2)
                    if last and j == 3 + 2 * KG:
                        sp.wait_ge(proj_done, g * TPG + (3 + 2 * KG))
                        load_ctx(0)
                        load_ctx(1)

            with sp.Fori(0, G - 1) as g:
                group(g, False)
            group(G - 1, True)

            sp.wait_ge(out_added, ALL_OUT + KD)
            sp.dma_start(scale_raw, scales).then_inc(scale_in, 16)
            sp.dma_start(lo_row[:], lo_rows).then_inc(scale_in, 16)
            sp.dma_start(gw[:], gate_w.rearrange("(k p) e -> p k e", p=P)).then_inc(ffn_in, 16)
            sp.dma_start(fb[:], ffn_bias).then_inc(ffn_in, 16)
            sp.wait_ge(scale_done, 1)
            sp.dma_start(wff_raw[:], w_ffn).then_inc(wff_in, 16)
            for b in range(2, NB):
                if b == 2:
                    sp.wait_ge(sq_mm, 1)
                else:
                    sp.wait_ge(xo_mm, b - 2)
                load_ctx(b)
            for o in range(KD):
                sp.wait_ge(f_done, 2 * o + 2)
                sp.dma_start(out[o * P:(o + 1) * P, :], acc[:, o, :]).then_inc(stored, 16)
            sp.wait_ge(stored, 16 * KD)

        @block.tensor
        def _(pe):
            pe.wait_ge(ones_set, 1)
            for k in range(KD):
                if k % 2 == 0:
                    pe.wait_ge(x_in[k // 2], 16)
                for s in range(2):
                    mm = pe.matmul(pY[:, s, 0:TH], ones[:], acc[:, k, s * TH:(s + 1) * TH],
                                   start=(k == 0), stop=(k == KD - 1))
            mm.then_inc(x_mean, 1)
            for b in range(NB):
                pe.wait_ge(x_summed, b + 1)
                mm = pe.matmul(pA[0:S, 0, b:b + 1], pre_x[:, b, :], ones[:, 0:1], start=True, stop=True)
            mm.then_inc(x_sq_mm, 1)
            for n in range(2):
                for s in range(2):
                    pe.wait_ge(x_diag, 2 * n + s + 1)
                    mm = pe.matmul([pY, pA][n][:, s, 0:TH], ones[0:S, :], [hid, gate][n][0:S, s * TH:(s + 1) * TH],
                                   start=True, stop=True)
                mm.then_inc(x_bc, 1)

            def products(ps, n_slot, r_hi, r_lo, k):
                passes = [(w_hi, r_hi), (w_hi, r_lo), (w_lo, r_hi)]
                for i, (w, r) in enumerate(passes):
                    for s in range(2):
                        mm = pe.matmul(ps[:, s, 0:TH], w[n_slot][:, k, :], r[:, k, s * TH:(s + 1) * TH],
                                       start=(k == 0 and i == 0), stop=(k == KD - 1 and i == 2))
                return mm

            pe.wait_ge(w_lo_done, 1)
            for k in range(KD):
                pe.wait_ge(h_lo_done[k % 2], k // 2 + 1)
                mm = products(pB, 0, h_hi, h_lo, k)
            mm.then_inc(proj_done, 1)
            pe.wait_ge(const_in, 16 * 9)
            for n in range(4):
                pe.wait_ge(dt_own, 2 + n // 2)
                if n >= 2:
                    pe.wait_ge(dt_copy, n - 1)
                src = [gate, hid][n // 2]
                for b in range(HB):
                    t0 = (n % 2 * HB + b) * S
                    mm = pe.transpose([pT, pS][n % 2][0:S, b * P:(b + 1) * P], src[:, t0:t0 + S], ident[:])
                mm.then_inc(dt_tr, 1)
            pe.wait_ge(dt_copy, 4)
            for b in range(NB):
                mm = pe.matmul(pY[:, b // HB, (b % HB) * S:(b % HB + 1) * S], da_t(b), tri[:],
                               start=True, stop=True)
            mm.then_inc(cs_mm, 1)

            def project(g, t, r_hi, r_lo, ks, fillers=None, before=None):
                if 0 in ks:
                    pe.wait_ge(w_lo_done, g * TPG + (t + 2))
                    free_bank(g, t)
                for k in ks:
                    if before is not None:
                        before(k)
                    mm = products(bank(t), (t + 1) % 2, r_hi, r_lo, k)
                    if k == KD - 1:
                        mm.then_inc(proj_done, 1)
                    for f in (fillers or {}).get(k, []):
                        f()

            def free_bank(g, t):
                o = t - (2 + 2 * KG)
                if t < 2:
                    pe.wait_ge(out_scaled, g * KD + (KD - 1 + t))
                elif t < 4:
                    pe.wait_ge(conv_done, g * (CST * CPG) + CST * (t - 1))
                elif t % 2 == 0 and o <= 0:
                    pe.wait_ge(conv_done, g * (CST * CPG) + CST * (t // 2 + 1))
                elif o <= 1:
                    pe.wait_ge(gated, g * KG + (t - 3) // 2)
                elif o == 2:
                    pe.wait_ge(skip_done, g * KG + (KG + 1))
                else:
                    pe.wait_ge(out_scaled, g * KD + (KD + o - 2))

            def seg(g, q, n):
                s = n // 2
                if n % 2 == 0:
                    pe.wait_ge(seg_in[s], g * (48 * KG) + 48 * (q + 1))
                pe.wait_ge(exp_done, g * (4 * KG) + (4 * q + n + 1))
                for j in range(2):
                    b = n % 2 * 2 + j
                    mm = pe.matmul(pS[0:S, 2 * j * S:2 * (j + 1) * S], seg_l[s][:, b, :], seg_r[s][:, b, :, :],
                                   start=True, stop=True)
                mm.then_inc(seg_mm, 1)

            def turn(g, q, s):
                if s == 0:
                    pe.wait_ge(silu_done, g * CPG + (q + 3))
                    if q == 0:
                        pe.wait_ge(cb_copy, g * 2 + 2)
                    else:
                        pe.wait_ge(hc_done, g * (2 * KG) + (2 * q + 1))
                else:
                    pe.wait_ge(hc_done, g * (2 * KG) + (2 * q + 2))
                for b in range(HB):
                    t0 = (s * HB + b) * S
                    mm = pe.transpose(pT[0:S, b * P:(b + 1) * P], hid[:, t0:t0 + S], ident[:])
                mm.then_inc(tr_done, 1)

            def cb(g, s):
                pe.wait_ge(silu_done, g * CPG + 2)
                if s == 0:
                    pe.wait_ge(hc_done, g * (2 * KG) + 1)
                else:
                    pe.wait_ge(cb_copy, g * 2 + 1)
                for b in range(HB):
                    t0 = (s * HB + b) * S
                    mm = pe.matmul(pT[0:S, b * S:(b + 1) * S], cB[:, t0:t0 + S], cC[:, t0:t0 + S],
                                   start=True, stop=True)
                mm.then_inc(cb_mm, 1)

            def y_product(g, q, s):
                if s == 0:
                    pe.wait_ge(skip_done, g * KG + (q + 1))
                pe.wait_ge(m_done, g * (2 * KG) + (2 * q + s + 1))
                pe.wait_ge(hc_done, g * (2 * KG) + (2 * q + s + 2))
                for b in range(HB):
                    for hh in range(2):
                        mm = pe.matmul(pY[hh * HP:(hh + 1) * HP, s, b * S:(b + 1) * S],
                                       hc[:, s * HB + b, hh * HP:(hh + 1) * HP],
                                       m_t[0:S, s * HB + b, hh, :], start=True, stop=True)
                mm.then_inc(y_mm, 1)

            def group(g):
                def F(f, *a):
                    return lambda: f(g, *a)
                w, yk = (h_hi, h_lo), (y_hi, y_lo)
                project(g, 0, *w, range(KD))
                project(g, 1, *w, range(KD))
                for q in range(KG):
                    if q == 0:
                        hf = {6: [F(cb, 0)]}
                        gf = {2: [F(cb, 1), F(seg, q, 0)], 4: [F(seg, q, 1)], 5: [F(seg, q, 2)], 6: [F(seg, q, 3)]}
                    else:
                        hf = {1: [F(turn, q - 1, 0)], 3: [F(turn, q - 1, 1)],
                              4: [F(y_product, q - 1, 0)], 5: [F(y_product, q - 1, 1)]}
                        gf = {1: [F(seg, q, 0)], 3: [F(seg, q, 1)], 5: [F(seg, q, 2)], 6: [F(seg, q, 3)]}
                    project(g, 2 + 2 * q, *w, range(KD), hf)
                    project(g, 3 + 2 * q, *w, range(KD), gf)
                o0 = 2 + 2 * KG
                q = KG - 1

                def y_ready(k):
                    pe.wait_ge(yl_done, g * KG + (k + 1))
                project(g, o0, *yk, range(KD - 1), {0: [F(turn, q, 0)], 3: [F(turn, q, 1)],
                                                    4: [F(y_product, q, 0)], 5: [F(y_product, q, 1)]}, y_ready)
                project(g, o0 + 1, *yk, range(4))
                project(g, o0, *yk, [KD - 1], before=y_ready)
                project(g, o0 + 1, *yk, range(4, KD))

                def gn_sums():
                    pe.wait_ge(sum_done, g * (KG - 1) + (KG - 1))
                    for b in range(NB):
                        mm = pe.matmul(pS[0:S, b:b + 1], ssum[:, b * S:(b + 1) * S], ones[:, 0:1],
                                       start=True, stop=True)
                    mm.then_inc(gn_mm, 1)

                def gn_spread():
                    for s in range(2):
                        pe.wait_ge(gn_diag, g * 2 + s + 1)
                        mm = pe.matmul([pT, pS][s][:, 0:TH], ones[0:S, :], diag[0:S, s * TH:(s + 1) * TH],
                                       start=True, stop=True)
                    mm.then_inc(gn_bc, 1)
                for o in range(2, KD):
                    project(g, o0 + o, *yk, range(KD), {0: [gn_sums], 5: [gn_spread]} if o == 2 else None)

            with pe.Fori(0, G) as g:
                group(g)

            pe.wait_ge(out_scaled, ALL_OUT + KD - 2)
            for k in range(KD):
                pe.wait_ge(out_added, ALL_OUT + k + 1)
                for s in range(2):
                    mm = pe.matmul(pY[:, s, 0:TH], ones[:], acc[:, k, s * TH:(s + 1) * TH],
                                   start=(k == 0), stop=(k == KD - 1))
            mm.then_inc(mean_mm, 1)

            def scores(b):
                pe.wait_ge(ctx_in[b % 3], 32 * (b // 3 + 1))
                if b < 2:
                    pe.wait_ge(centred, b + 1)
                else:
                    pe.wait_ge(pt_copy, b - 1)
                for k in range(KD):
                    mm = pe.matmul([pT, pS][b % 2][0:S, 0:LK], h[:, k, cols(b)], ctx_cols[b % 3][:, k, :],
                                   start=(k == 0), stop=(k == KD - 1))
                mm.then_inc(sc_mm, 1)

            def turn_probs(b):
                pe.wait_ge(pn_done, b + 1)
                for c in range(CK):
                    mm = pe.transpose([pT, pS][b % 2][0:LC, c * S:(c + 1) * S], prob[b % 2][:, c * LC:(c + 1) * LC],
                                      ident[0:S, 0:S])
                mm.then_inc(pt_mm, 1)

            def attend(b):
                pe.wait_ge(pt_copy, b + 1)
                if b >= 2:
                    pe.wait_ge(x2_done, b - 1)
                for d in range(KD):
                    for c in range(CK):
                        mm = pe.matmul([pY, pB][b % 2][:, d // 4, (d % 4) * S:(d % 4 + 1) * S],
                                       ctx_rows[b % 3][:, c, d * P:(d + 1) * P], prob_t[b % 2][:, c, :],
                                       start=(c == 0), stop=(c == CK - 1))
                mm.then_inc(xo_mm, 1)

            def mean_2(b):
                pe.wait_ge(pre_done, b + 1)
                if b >= 1:
                    pe.wait_ge(centred2, b)
                pe.matmul(mean2, ones[:], pre[:, b % 2, :], start=True, stop=True).then_inc(mean2_mm, 1)

            def route_2(b):
                pe.wait_ge(centred2, b + 1)
                for k in range(KD):
                    pe.matmul(logits[:, b, :], h[:, k, cols(b)], gw[:, k, :], start=(k == 0), stop=(k == KD - 1))
                pe.wait_ge(pre_sq_done, b + 1)
                pe.matmul(sums_sq[:, 1, b:b + 1], pre_sq[:, b % 2, :], ones[:, 0:1], start=True, stop=True)\
                    .then_inc(sq2_mm, 1)

            def ffn_k(o, k):
                if o == 0:
                    pe.wait_ge(sign_done, KD)
                    pe.wait_ge(r_turned, 2)
                    pe.wait_ge(xs_hi_done, k + 1)
                for x in (xs_hi, xs_lo):
                    if o == 0 and x is xs_lo:
                        pe.wait_ge(xs_lo_done, k + 1)
                    for s in range(2):
                        mm = pe.matmul(f_bank(o, s), wff[:, k, o * P:(o + 1) * P], x[:, k, s * TH:(s + 1) * TH],
                                       start=(k == 0 and x is xs_hi), stop=(k == KD - 1 and x is xs_lo))
                if k == KD - 1:
                    mm.then_inc(f_mm, 1)

            scores(0)
            scores(1)
            for b in range(NB):
                pe.wait_ge(squares_summed, b + 1)
                mm = pe.matmul(sums_sq[:, 0, b:b + 1], pre_1[:, b, :], ones[:, 0:1], start=True, stop=True)
            mm.then_inc(sq_mm, 1)
            pe.wait_ge(ffn_in, 32)
            for b in range(NB):
                if b >= 1 and b + 1 < NB:
                    scores(b + 1)
                turn_probs(b)
                if b >= 2:
                    route_2(b - 2)
                if b >= 1:
                    mean_2(b - 1)
                attend(b)
            route_2(NB - 2)
            mean_2(NB - 1)
            route_2(NB - 1)

            pe.wait_ge(r_lo, 2)
            pe.wait_ge(r_hi, 2)
            pe.wait_ge(x2_done, NB)
            for n in range(2):
                for s in range(2):
                    for b in range(HB):
                        dst = [[pT, pS][s], pY[:, s]][n][0:NE3, b * S:(b + 1) * S]
                        mm = pe.transpose(dst, route3[:, n, s * HB + b, :].bitcast(F32), ident[0:S, 0:S])
                mm.then_inc(r_tr, 1)
            pe.wait_ge(scale_done, 1)
            def in_scale(k):
                pe.wait_ge(r_copy, 2)
                if k >= 2:
                    pe.wait_ge(xs_done, k - 1)
                for s in range(2):
                    mm = pe.matmul(pAB[k % 2][:, s, 0:TH], scale3[:, 0, k * P:(k + 1) * P],
                                   route_t[:, 0, s * TH:(s + 1) * TH], start=True, stop=True)
                mm.then_inc(is_mm, 1)

            def out_scale(o):
                if o == 0:
                    pe.wait_ge(xs_done, KD)
                else:
                    pe.wait_ge(os_copy, o)
                for s in range(2):
                    mm = pe.matmul(pA[:, s, 0:TH], scale3[:, 1, o * P:(o + 1) * P],
                                   route_t[:, 1, s * TH:(s + 1) * TH], start=True, stop=True)
                mm.then_inc(os_mm, 1)

            in_scale(0)
            in_scale(1)
            for k in range(KD):
                if k + 2 < KD:
                    in_scale(k + 2)
                ffn_k(0, k)
                ffn_k(1, k)
            out_scale(0)
            for o in range(2, KD):
                if o >= 3:
                    pe.wait_ge(f_scaled, 2 * (o - 2))
                for k in range(KD):
                    ffn_k(o, k)
                    if o == 2 and k == KD // 2:
                        out_scale(1)
                out_scale(o)

        @block.scalar
        def _(act):
            for b in range(NB):
                act.wait_ge(x_centred, b + 1)
                nc.scalar.activation(x_sq[:, :, cols(b)], xc[:, :, cols(b)], ACT.Square).then_inc(x_squared, 1)

            def split_hi(slot, tile, tiles_done=None):
                act.wait_ge(w_in[slot], tile)
                if tiles_done is not None:
                    act.wait_ge(proj_done, tiles_done)
                nc.scalar.copy(w_hi[slot][:], w_raw[slot][:]).then_inc(w_hi_done, 1)

            split_hi(0, 16)
            split_hi(1, 16)
            for n in range(2):
                act.wait_ge(x_stat, [1, 5][n])
                nc.scalar.activation(x_small[:, 1 + 4 * n, :], x_small[:, 4 * n, :], ACT.Sqrt).then_inc(x_std, 1)
            for k in range(KD):
                act.wait_ge(ln_out, k + 1)
                nc.scalar.copy(h_hi[:, k, :], x_sq[:, k, :]).then_inc(h_hi_done, 1)
                if k == 0:
                    act.wait_ge(x_bc, 2)
                    nc.scalar.copy(flat(ssum), halves(pA)).then_inc(std_copy, 1)
            act.wait_ge(const_in, 16 * 9)
            nc.scalar.activation(hexp[:], hpar[:, 1:2], ACT.Exp).then_inc(dt_act, 1)
            act.wait_ge(proj_done, 1)
            nc.scalar.activation(flat(th), halves(pB), ACT.Abs, bias=hpar[:, 0:1]).then_inc(dt_abs, 1)
            act.wait_ge(dt_abs, 1)
            nc.scalar.activation(th[:], th[:], ACT.Exp, scale=-1.0).then_inc(dt_act, 1)
            act.wait_ge(dt_act, 2)
            nc.scalar.activation(th[:], th[:], ACT.Ln, bias=1.0).then_inc(dt_act, 1)
            act.wait_ge(cs_split, 3)
            nc.scalar.mul(cs_parts(1), cs_parts(0), -1.0).then_inc(cs_negd, 1)

            act.wait_ge(halved, 1)

            def group(g):
                def split(t):
                    split_hi(t % 2, g * (8 * TPG) + 16 * (t // 2 + 2), g * TPG + (t + 1))

                def conv_tap(c, buf, t):
                    act.wait_ge(proj_done, g * TPG + (t + 2))
                    if c >= 2:
                        act.wait_ge(yg_done, g * KG + (c - 1))
                    w = par[:, bass.ds(g * CPG + c, 1), :].squeeze(1)
                    nc.scalar.activation(flat(buf), halves(bank(t)), ACT.Identity, bias=w[:, CONV:CONV + 1],
                                         scale=w[:, CONV - 1:CONV]).then_inc(conv_done, 1)

                def conv_tanh(c, buf):
                    act.wait_ge(conv_done, g * (CST * CPG) + CST * (c + 1))
                    if c:
                        act.wait_ge(silu_done, g * CPG + c)
                    else:
                        act.wait_ge(out_added, g * KD + KD)
                    nc.scalar.activation(th[:], buf[:, :], ACT.Tanh).then_inc(tanh_c, 1)

                def gate_tanh(q):
                    act.wait_ge(proj_done, g * TPG + (5 + 2 * q))
                    if q:
                        act.wait_ge(sq_done, g * KG + q)
                        act.wait_ge(yl_done, g * KG + q)
                    nc.scalar.activation(flat(gate), halves(pB), ACT.Tanh, scale=0.5).then_inc(tanh_g, 1)

                def exps(q, n):
                    act.wait_ge(seg_mm, g * (4 * KG) + (4 * q + n + 2))
                    nc.scalar.activation(m_t[0:S, 2 * n:2 * n + 2].rearrange("p b h i -> p (b h i)"),
                                         pS[0:S, 0:4 * S], ACT.Exp).then_inc(exp_done, 1)

                def y_out(q):
                    act.wait_ge(yg_done, g * KG + (q + 2))
                    if q == 0:
                        act.wait_ge(acc_ln, KD)
                    w = par[:, bass.ds(g * CPG + (2 + q), 1), :].squeeze(1)
                    nc.scalar.activation(y_hi[:, q, :], gate[:], ACT.Copy, scale=w[:, NPAR - 1:NPAR])\
                        .then_inc(y_done, 1)
                    if q >= 2:
                        act.wait_ge(sum_done, g * (KG - 1) + (q - 1))
                    nc.scalar.activation((sq if q else ssum)[:], gate[:], ACT.Square).then_inc(sq_done, 1)

                split(0)
                conv_tap(0, cB, 0)
                split(1)
                conv_tanh(0, cB)
                conv_tap(1, cC, 1)
                split(2)
                conv_tanh(1, cC)
                for q in range(KG):
                    if q:
                        split(2 + 2 * q)
                        gate_tanh(q - 1)
                        y_out(q - 1)
                    split(3 + 2 * q)
                    conv_tap(2 + q, hid, 2 + 2 * q)
                    exps(q, 0)
                    exps(q, 1)
                    exps(q, 2)
                    conv_tanh(2 + q, hid)
                    exps(q, 3)
                o0 = 2 + 2 * KG
                split(o0)
                gate_tanh(KG - 1)
                y_out(KG - 1)
                split(o0 + 1)
                act.wait_ge(gn_var, g + 1)
                nc.scalar.activation(small[:], small[:], ACT.Sqrt).then_inc(gn_std, 1)
                split(o0 + 2)
                act.wait_ge(gn_bc, g + 1)
                for s in range(2):
                    nc.scalar.copy(flat(rs)[:, s], [pT, pS][s][:, 0:TH]).then_inc(gn_rs, 1)
                for o in range(3, KD):
                    split(o0 + o)

            with act.Fori(0, G) as g:
                group(g)

            act.wait_ge(scale_in, 32)
            nc.scalar.copy(scale3[:].rearrange("p n d -> p (n d)"), scale_raw).then_inc(scale_hi, 1)
            act.wait_ge(scale_x, 1)
            nc.scalar.copy(scale3[:].rearrange("p n d -> p (n d)"), scale_tmp).then_inc(scale_done, 1)
            for b in range(NB):
                act.wait_ge(centred, b + 1)
                nc.scalar.activation(y[:, :, cols(b)], h[:, :, cols(b)], ACT.Square).then_inc(squared, 1)
            act.wait_ge(var_done, 1)
            nc.scalar.activation(stat[:, 3, :], stat[:, 3, :], ACT.Sqrt).then_inc(std_done, 1)

            def softmax(b):
                act.wait_ge(mx_done, b + 1)
                if b >= 2:
                    act.wait_ge(pt_mm, b - 1)
                nc.scalar.activation(prob[b % 2][:], [pT, pS][b % 2][0:S, 0:LK], ACT.Exp, bias=stat[:, 0, b:b + 1],
                                     scale=stat[:, 4, b:b + 1], accum_out=stat[:, 1, b:b + 1]).then_inc(ex_done, 1)

            def squares_2(b):
                act.wait_ge(centred2, b + 1)
                if b >= 2:
                    act.wait_ge(pre_sq_done, b - 1)
                nc.scalar.activation(sq2[b % 2][:], h[:, :, cols(b)], ACT.Square).then_inc(squared2, 1)

            softmax(0)
            for b in range(NB):
                if b + 1 < NB:
                    softmax(b + 1)
                else:
                    act.wait_ge(wff_in, 16)
                    for k in range(KD):
                        nc.scalar.activation(wff[:, k, :], wff_raw[:, k, :], ACT.Sign).then_inc(sign_done, 1)
                if b >= 1:
                    squares_2(b - 1)
            squares_2(NB - 1)

            act.wait_ge(r_own, 1)
            nc.scalar.activation(rstat[:, 1, :], rstat[:, 0, :], ACT.Sqrt).then_inc(r_std, 1)
            act.wait_ge(r_own, 5)
            nc.scalar.activation(route[:, 0], route[:, 1], ACT.Exp).then_inc(r_exp, 1)
            act.wait_ge(r_own, 9)
            for i in range(2):
                nc.scalar.copy(route3[:, :, :, i * NE:(i + 1) * NE], route[:]).then_inc(r_hi, 1)
            act.wait_ge(r_tr, 2)
            for s in range(2):
                nc.scalar.copy(route_t[:, 1, s * TH:(s + 1) * TH], pY[0:NE3, s, 0:TH]).then_inc(r_turned, 1)
            for k in range(KD):
                act.wait_ge(xs_done, k + 1)
                nc.scalar.copy(xs_hi[:, k, :], h[:, k, :]).then_inc(xs_hi_done, 1)
            for o in range(KD):
                act.wait_ge(os_mm, o + 1)
                if o >= 3:
                    act.wait_ge(f_done, 2 * (o - 2))
                nc.scalar.copy(flat(oscale[o % 3]), halves(pA)).then_inc(os_copy, 1)

        @block.gpsimd
        def _(pool):
            nc.gpsimd.memset(ones[:], 1.0).then_inc(ones_set, 1)
            for k in range(1, KD, 2):
                pool.wait_ge(h_hi_done, k + 1)
                nc.gpsimd.tensor_tensor(h_lo[:, k, :], x_sq[:, k, :], h_hi[:, k, :].bitcast(F32), ALU.subtract)\
                    .then_inc(h_lo_done[1], 1)
            pool.wait_ge(std_copy, 1)
            for k in range(KD):
                pool.wait_ge(ln_out, k + 1)
                nc.gpsimd.tensor_tensor(xc[:, k, :], xc[:, k, :], ssum[:], ALU.mult).then_inc(x_tmp, 1)
                pool.wait_ge(x_tmp, k + 1)
                nc.gpsimd.tensor_tensor(acc[:, k, :], acc[:, k, :], xc[:, k, :], ALU.add).then_inc(acc_ln, 1)
            pool.wait_ge(acc_ln, KD)

            def group(g):
                for q in range(1, KG):
                    pool.wait_ge(sq_done, g * KG + (q + 1))
                    if q >= 2:
                        pool.wait_ge(sum_done, g * (KG - 1) + (q - 1))
                    nc.gpsimd.tensor_tensor(ssum[:], ssum[:], sq[:], ALU.add).then_inc(sum_done, 1)
                for o in range(KD):
                    pool.wait_ge(out_scaled, g * KD + (KD + o + 1))
                    nc.gpsimd.tensor_tensor(acc[:, o, :], acc[:, o, :], tmp[o % 2][:], ALU.add).then_inc(out_added, 1)

            with pool.Fori(0, G) as g:
                group(g)

        @block.vector
        def _(v):
            stt = nc.vector.scalar_tensor_tensor
            tt = nc.vector.tensor_tensor
            ts = nc.vector.tensor_scalar

            def centre_batch(b, dst, mean, done):
                stt(dst[:, :, cols(b)], bc(mean.unsqueeze(1), [P, KD, S]), -1.0 / D, acc[:, :, cols(b)],
                    ALU.mult, ALU.add).then_inc(done, 1)

            def sum_tiles(dst, src, done):
                nc.vector.tensor_reduce(dst, src.rearrange("p k i -> p i k"), AX.X, ALU.add).then_inc(done, 1)

            def split_lo(slot, tiles):
                v.wait_ge(w_hi_done, tiles)
                tt(w_lo[slot][:], w_raw[slot][:], w_hi[slot][:].bitcast(F32), ALU.subtract).then_inc(w_lo_done, 1)

            def flat3(buf, k):
                return buf[:, k, :].rearrange("p (s n) -> p s n", s=2)

            def spread(dst, s, src):
                return tt(dst[0:S, s * TH:(s + 1) * TH].rearrange("p (b i) -> p b i", b=HB),
                          bc(ident[0:S, 0:S].unsqueeze(1), [S, HB, S]), bc(src.unsqueeze(2), [S, HB, S]), ALU.mult)

            v.sem_inc(out_scaled, KD)
            v.sem_inc(out_added, KD)
            v.sem_inc(skip_done, 1)
            v.sem_inc(exp_done, 1)
            v.sem_inc(hc_done, 1)
            v.sem_inc(yg_done, 1)
            v.sem_inc(seg_mm, 1)
            v.wait_ge(x_mean, 1)
            for b in range(NB + 2):
                if b < NB:
                    centre_batch(b, xc, pY[:, b // HB, (b % HB) * S:(b % HB + 1) * S], x_centred)
                if b >= 2:
                    v.wait_ge(x_squared, b - 1)
                    sum_tiles(pre_x[:, b - 2, :], x_sq[:, :, cols(b - 2)], x_summed)
            st = [x_small[:, i, :] for i in range(7)]
            v.wait_ge(x_sq_mm, 1)
            ts(st[0], pA[0:S, 0, 0:NB], 1.0 / D, EPS, ALU.mult, ALU.add).then_inc(x_stat, 1)
            v.wait_ge(x_std, 1)
            nc.vector.reciprocal(st[2], st[1]).then_inc(x_stat, 1)
            v.wait_ge(x_stat, 2)
            tt(st[3], st[2], st[2], ALU.mult).then_inc(x_stat, 1)
            v.wait_ge(x_stat, 3)
            stt(st[6], pA[0:S, 0, 0:NB], 1.0 / D, st[3], ALU.mult, ALU.mult).then_inc(x_stat, 1)
            v.wait_ge(x_stat, 4)
            ts(st[4], st[6], EPS, None, ALU.add).then_inc(x_stat, 1)
            v.wait_ge(x_std, 2)
            nc.vector.reciprocal(st[6], st[5]).then_inc(x_stat, 1)
            v.wait_ge(x_stat, 6)
            tt(st[3], st[6], st[2], ALU.mult).then_inc(x_stat, 1)
            v.wait_ge(x_stat, 7)
            v.wait_ge(const_in, 16 * 9)
            for n in range(2):
                for s in range(2):
                    spread([hid, gate][n], s, st[[3, 2][n]][:, s * HB:(s + 1) * HB]).then_inc(x_diag, 1)
            for i in range(2):
                split_lo(i, i + 1)

            def h_split(k):
                v.wait_ge(h_hi_done, k + 1)
                tt(h_lo[:, k, :], x_sq[:, k, :], h_hi[:, k, :].bitcast(F32), ALU.subtract).then_inc(h_lo_done[0], 1)
            v.wait_ge(x_bc, 1)
            for k in range(KD):
                stt(flat3(x_sq, k), flat3(xc, k), nw[:, k:k + 1], halves(pY), ALU.mult, ALU.mult).then_inc(ln_out, 1)
                if k % 2:
                    h_split(k - 1)
            ts(par[:, :, 0:CONV + 1], par[:, :, 0:CONV + 1], 0.5, None, ALU.mult).then_inc(dt_own, 1)
            ts(par[:, :, NPAR - 1:NPAR], par[:, :, NPAR - 1:NPAR], 0.5, None, ALU.mult).then_inc(halved, 1)

            v.wait_ge(proj_done, 1)
            v.wait_ge(dt_abs, 1)
            ts(flat(gate), halves(pB), hpar[:, 0:1], 0.0, ALU.add, ALU.max).then_inc(dt_max, 1)
            v.wait_ge(dt_act, 3)
            v.wait_ge(dt_max, 1)
            tt(gate[:], gate[:], th[:], ALU.add).then_inc(dt_own, 1)
            v.wait_ge(dt_own, 2)
            ts(hid[:], gate[:], hexp[:, 0:1], -1.0, ALU.mult, ALU.mult).then_inc(dt_own, 1)
            for n in range(4):
                v.wait_ge(dt_tr, n + 1)
                src = [pT, pS][n % 2][0:S, :]
                dst = dt_tok[:].rearrange("p b h -> p (b h)") if n < 2 else m_flat[0:S]
                nc.vector.tensor_copy(dst[:, n % 2 * HB * P:(n % 2 + 1) * HB * P], src).then_inc(dt_copy, 1)
            v.wait_ge(cs_mm, 1)
            parts = [cs_parts(0)[:, c * T:(c + 1) * T] for c in range(3)]
            nc.vector.tensor_copy(flat(sq), halves(pY)).then_inc(dt_own, 1)
            v.wait_ge(dt_own, 4)
            nc.vector.tensor_copy(parts[0], sq[:]).then_inc(cs_split, 1)
            v.wait_ge(cs_split, 1)
            tt(sq[:], sq[:], parts[0], ALU.subtract).then_inc(dt_own, 1)
            v.wait_ge(dt_own, 5)
            nc.vector.tensor_copy(parts[1], sq[:]).then_inc(cs_split, 1)
            v.wait_ge(cs_split, 2)
            tt(sq[:], sq[:], parts[1], ALU.subtract).then_inc(dt_own, 1)
            v.wait_ge(dt_own, 6)
            nc.vector.tensor_copy(parts[2], sq[:]).then_inc(cs_split, 1)
            v.wait_ge(cs_negd, 1)
            v.wait_ge(halved, 1)

            def group(g):
                def split(t):
                    split_lo(t % 2, g * TPG + (t + 3))

                def taps(c, buf, t):
                    w = par[:, bass.ds(g * CPG + c, 1), :].squeeze(1)
                    for n in range(1, CONV):
                        for s in range(2):
                            v.wait_ge(conv_done, g * (CST * CPG) + (CST * c + (1 if n == 1 else 2 * n - 2 + s)))
                            stt(shifted(buf, n)[:, s], batches(bank(t))[:, s, :, 0:S - n],
                                w[:, CONV - 1 - n:CONV - n], shifted(buf, n)[:, s], ALU.mult, ALU.add)\
                                .then_inc(conv_done, 1)

                def silu(c, buf):
                    v.wait_ge(tanh_c, g * CPG + (c + 1))
                    stt(buf[:, :], th[:], 1.0, buf[:, :], ALU.add, ALU.mult).then_inc(silu_done, 1)

                def cb_out(s):
                    v.wait_ge(cb_mm, g * 2 + (s + 1))
                    nc.vector.tensor_copy(g_t[:, s * HB:(s + 1) * HB, :].rearrange("p b i -> p (b i)"),
                                          pT[0:S, 0:TH]).then_inc(cb_copy, 1)

                def gate_out(q):
                    v.wait_ge(tanh_g, g * KG + (q + 1))
                    stt(flat(gate), flat(gate), 1.0, halves(pB), ALU.add, ALU.mult).then_inc(gated, 1)

                def tokens_out(q, s):
                    if q == 0 and s == 0:
                        v.wait_ge(dt_in, g * 16 + 16)
                    v.wait_ge(tr_done, g * (2 * KG) + (2 * q + s + 1))
                    bs = slice(s * HB, (s + 1) * HB)
                    tt(hc[:, bs, :].rearrange("p b (h c) -> p b h c", h=2),
                       pT[0:S, :].rearrange("p (b h c) -> p b h c", b=HB, h=2),
                       bc(dt_g[:, bs, 2 * q:2 * q + 2].unsqueeze(3), [S, HB, 2, HP]),
                       ALU.mult).then_inc(hc_done, 1)

                def decay(q, s):
                    if q == 0 and s == 0:
                        v.wait_ge(cb_copy, g * 2 + 2)
                    v.wait_ge(exp_done, g * (4 * KG) + (4 * q + 2 * s + 3))
                    bs = slice(s * HB, (s + 1) * HB)
                    tt(m_t[0:S, bs], m_t[0:S, bs], bc(g_t[:, bs, :].unsqueeze(2), [S, HB, 2, S]),
                       ALU.mult).then_inc(m_done, 1)

                def skip(q):
                    v.wait_ge(y_mm, g * (2 * KG) + (2 * q + 2))
                    w = par[:, bass.ds(g * CPG + (2 + q), 1), :].squeeze(1)
                    stt(flat(hid), flat(hid), w[:, CONV + 1:CONV + 2], halves(pY), ALU.mult, ALU.add)\
                        .then_inc(skip_done, 1)

                def gate_y(q):
                    v.wait_ge(skip_done, g * KG + (q + 2))
                    tt(gate[:], gate[:], hid[:], ALU.mult).then_inc(yg_done, 1)

                def y_low(q):
                    v.wait_ge(y_done, g * KG + (q + 1))
                    w = par[:, bass.ds(g * CPG + (2 + q), 1), :].squeeze(1)
                    stt(y_lo[:, q, :], gate[:], w[:, NPAR - 1:NPAR], y_hi[:, q, :].bitcast(F32), ALU.mult,
                        ALU.subtract).then_inc(yl_done, 1)

                def y_steps(q):
                    gate_out(q)
                    tokens_out(q, 0)
                    decay(q, 0)
                    tokens_out(q, 1)
                    decay(q, 1)
                    skip(q)
                    gate_y(q)

                split(0)
                taps(0, cB, 0)
                split(1)
                silu(0, cB)
                taps(1, cC, 1)
                split(2)
                silu(1, cC)
                for q in range(KG):
                    if q:
                        split(2 + 2 * q)
                        y_steps(q - 1)
                        y_low(q - 1)
                    split(3 + 2 * q)
                    if q == 0:
                        cb_out(0)
                    taps(2 + q, hid, 2 + 2 * q)
                    if q == 0:
                        cb_out(1)
                    silu(2 + q, hid)
                o0 = 2 + 2 * KG
                split(o0)
                y_steps(KG - 1)
                y_low(KG - 1)
                split(o0 + 1)
                v.wait_ge(gn_mm, g + 1)
                ts(small[:], pS[0:S, 0:NB], 0.25 / (DI // G), EPS, ALU.mult, ALU.add).then_inc(gn_var, 1)
                v.wait_ge(gn_std, g + 1)
                nc.vector.reciprocal(small[:], small[:]).then_inc(gn_r, 1)
                v.wait_ge(gn_r, g + 1)
                for s in range(2):
                    spread(diag, s, small[:, s * HB:(s + 1) * HB]).then_inc(gn_diag, 1)
                split(o0 + 2)
                v.wait_ge(gn_rs, g * 2 + 2)
                for o in range(KD):
                    t = o0 + o
                    if o >= 2 and t + 1 < TPG:
                        split(t + 1)
                    v.wait_ge(proj_done, g * TPG + (t + 2))
                    if o >= 2:
                        v.wait_ge(out_added, g * KD + (KD + o - 1))
                    else:
                        v.wait_ge(sum_done, g * (KG - 1) + (KG - 1))
                    tt(flat(tmp[o % 2]), halves(bank(t)), flat(rs), ALU.mult).then_inc(out_scaled, 1)

            with v.Fori(0, G) as g:
                group(g)

            v.wait_ge(scale_hi, 1)
            stt(scale_tmp, scale3[:].rearrange("p n d -> p (n d)").bitcast(F32), lo_row[:, 0:1], scale_raw,
                ALU.mult, ALU.add).then_inc(scale_x, 1)
            v.wait_ge(mean_mm, 1)
            for b in range(NB + 2):
                if b < NB:
                    centre_batch(b, h, pY[:, b // HB, (b % HB) * S:(b % HB + 1) * S], centred)
                if b >= 2:
                    v.wait_ge(squared, b - 1)
                    sum_tiles(pre_1[:, b - 2, :], y[:, :, cols(b - 2)], squares_summed)
            v.wait_ge(sq_mm, 1)
            ts(stat[:, 3, :], sums_sq[:, 0, :], 1.0 / D, EPS, ALU.mult, ALU.add).then_inc(var_done, 1)
            v.wait_ge(std_done, 1)
            nc.vector.reciprocal(stat[:, 4, :], stat[:, 3, :]).then_inc(inv_std, 1)
            v.wait_ge(inv_std, 1)
            ts(stat[:, 5, :], stat[:, 4, :], -1.0, None, ALU.mult).then_inc(inv_std, 1)
            v.wait_ge(inv_std, 2)

            def score_max(b):
                v.wait_ge(sc_mm, b + 1)
                nc.vector.tensor_reduce(stat[:, 3, b:b + 1], [pT, pS][b % 2][0:S, 0:LK], AX.X, ALU.max).then_inc(mx_raw, 1)
                v.wait_ge(mx_raw, b + 1)
                tt(stat[:, 0, b:b + 1], stat[:, 3, b:b + 1], stat[:, 5, b:b + 1], ALU.mult).then_inc(mx_done, 1)

            def normalise(b):
                v.wait_ge(ex_done, b + 1)
                nc.vector.reciprocal(stat[:, 2, b:b + 1], stat[:, 1, b:b + 1]).then_inc(ri_done, 1)
                v.wait_ge(ri_done, b + 1)
                ts(prob[b % 2][:], prob[b % 2][:], stat[:, 2, b:b + 1], None, ALU.mult).then_inc(pn_done, 1)

            def turned(b):
                v.wait_ge(pt_mm, b + 1)
                nc.vector.tensor_copy(prob_t[b % 2][:].rearrange("p c i -> p (c i)"), [pT, pS][b % 2][0:LC, 0:CK * S])\
                    .then_inc(pt_copy, 1)

            def add_ctx(b):
                v.wait_ge(xo_mm, b + 1)
                xa = acc[:, :, cols(b)].rearrange("p (s d) i -> p s d i", s=2)
                tt(xa, batches([pY, pB][b % 2]), xa, ALU.add).then_inc(x2_done, 1)
                v.wait_ge(x2_done, b + 1)
                sum_tiles(pre[:, b % 2, :], acc[:, :, cols(b)], pre_done)

            def centre_2(b):
                v.wait_ge(mean2_mm, b + 1)
                centre_batch(b, h, mean2, centred2)

            def sum_squares_2(b):
                v.wait_ge(squared2, b + 1)
                if b >= 2:
                    v.wait_ge(sq2_mm, b - 1)
                sum_tiles(pre_sq[:, b % 2, :], sq2[b % 2][:], pre_sq_done)

            score_max(0)
            normalise(0)
            for b in range(NB):
                if b + 1 < NB:
                    score_max(b + 1)
                turned(b)
                if b >= 1:
                    centre_2(b - 1)
                if b + 1 < NB:
                    normalise(b + 1)
                if b >= 1:
                    sum_squares_2(b - 1)
                add_ctx(b)
            centre_2(NB - 1)
            sum_squares_2(NB - 1)

            def per_token(n, last=NE):
                return bc(rstat[:, n, :].unsqueeze(2), [S, NB, last])

            v.wait_ge(sq2_mm, NB)
            ts(rstat[:, 0, :], sums_sq[:, 1, :], 1.0 / D, EPS, ALU.mult, ALU.add).then_inc(r_own, 1)
            v.wait_ge(r_std, 1)
            nc.vector.reciprocal(rstat[:, 0, :], rstat[:, 1, :]).then_inc(r_own, 1)
            v.wait_ge(r_own, 2)
            tt(route[:, 0], logits, per_token(0), ALU.mult).then_inc(r_own, 1)
            v.wait_ge(r_own, 3)
            nc.vector.tensor_reduce(rstat[:, 2, :], route[:, 0], AX.X, ALU.max).then_inc(r_own, 1)
            v.wait_ge(r_own, 4)
            tt(route[:, 1], route[:, 0], per_token(2), ALU.subtract).then_inc(r_own, 1)
            v.wait_ge(r_exp, 1)
            nc.vector.tensor_reduce(rstat[:, 3, :], route[:, 0], AX.X, ALU.add).then_inc(r_own, 1)
            v.wait_ge(r_own, 6)
            nc.vector.reciprocal(rstat[:, 4, :], rstat[:, 3, :]).then_inc(r_own, 1)
            v.wait_ge(r_own, 7)
            tt(route[:, 1], route[:, 0], per_token(4), ALU.mult).then_inc(r_own, 1)
            v.wait_ge(r_own, 8)
            tt(route[:, 0], route[:, 1], per_token(0), ALU.mult).then_inc(r_own, 1)
            v.wait_ge(r_hi, 1)
            for n in range(2):
                tt(route3[:, n, :, 2 * NE:NE3], route[:, n], route3[:, n, :, 0:NE].bitcast(F32), ALU.subtract)\
                    .then_inc(r_lo, 1)
            v.wait_ge(r_tr, 1)
            for s in range(2):
                nc.vector.tensor_copy(route_t[:, 0, s * TH:(s + 1) * TH], [pT, pS][s][0:NE3, 0:TH]).then_inc(r_copy, 1)

            def xs_low(k):
                v.wait_ge(xs_hi_done, k + 1)
                tt(xs_lo[:, k, :], h[:, k, :], xs_hi[:, k, :].bitcast(F32), ALU.subtract).then_inc(xs_lo_done, 1)
            for k in range(KD):
                v.wait_ge(is_mm, k + 1)
                tt(flat3(h, k), flat3(h, k), halves(pAB[k % 2]), ALU.mult).then_inc(xs_done, 1)
                if k:
                    xs_low(k - 1)
            xs_low(KD - 1)
            for o in range(KD):
                v.wait_ge(f_mm, o + 1)
                v.wait_ge(os_copy, o + 1)
                for s in range(2):
                    half = oscale[o % 3][:, s * TH:(s + 1) * TH]
                    tt(half, f_bank(o, s), half, ALU.mult).then_inc(f_scaled, 1)
                for s in range(2):
                    v.wait_ge(f_scaled, 2 * o + s + 1)
                    half = acc[:, o, s * TH:(s + 1) * TH]
                    stt(half, oscale[o % 3][:, s * TH:(s + 1) * TH], fb[:, o:o + 1], half, ALU.add, ALU.add)\
                        .then_inc(f_done, 1)


def kernel(**inputs):
    import ml_dtypes
    import concourse.bacc as bacc
    from concourse.bass_utils import run_bass_kernel_spmd as run

    A = {k: np.asarray(v) for k, v in inputs.items()}
    L = "L0_attn_"

    def channels(v):
        return np.moveaxis(v.reshape(-1, P, *v.shape[1:]), 1, 0)

    w_in = A[L + "in_proj_w"].reshape(-1, P, KD, P).transpose(0, 3, 2, 1)
    w_out = A[L + "out_proj_w"].reshape(KD, P, G, KG, P).transpose(2, 0, 4, 3, 1)
    n_di = DI // P
    order = []
    for g in range(G):
        tiles = [w_in[2 * n_di + g], w_in[2 * n_di + G + g]]
        for q in range(KG):
            tiles += [w_in[n_di + g * KG + q], w_in[g * KG + q]]
        order += tiles + [w_out[g, o] for o in range(KD)]
    conv_w, conv_b = A[L + "conv_w"], A[L + "conv_b"]
    skip = np.repeat(A[L + "Dp"], HP)
    par_c = np.zeros((conv_w.shape[0], NPAR), np.float32)
    par_c[:, 0:CONV], par_c[:, CONV] = conv_w, conv_b
    par_c[:DI, CONV + 1], par_c[:DI, CONV + 2] = skip, A[L + "gnorm_w"]
    par_t = par_c.reshape(-1, P, NPAR)
    conv_tiles = [t for g in range(G) for t in [n_di + g, n_di + G + g] + list(range(g * KG, (g + 1) * KG))]
    par = np.stack([par_t[t] for t in conv_tiles], 1)

    const32 = np.zeros((P, P + S), np.float32)
    const32[:, :P] = np.eye(P)
    const32[:S, P:] = np.triu(np.ones((S, S)))
    bf = ml_dtypes.bfloat16
    seg_r0 = np.zeros((SEGK, HB, 2, S), np.float32)
    seg_r0[3:6, :, 0], seg_r0[6:9, :, 1] = 1, 1
    seg_r0[CSK:] = np.where(np.arange(S)[None, :] < np.arange(S)[:, None], MASKED, 0.0)[:, None, None, :]
    seg_l0 = np.zeros((SEGK, HB, S), np.float32)
    seg_l0[0:3] = 1
    seg_l0[CSK:] = np.eye(S)[:, None, :]

    lo_rows = np.zeros((NE3, 1), np.float32)
    lo_rows[NE:2 * NE] = -1

    arrays = {
        "x_t": A["x"].reshape(T, D).T,
        "w_main": np.stack([w_in[-1]] + order + order[:1]),
        "par": par,
        "norm_w": channels(A[L + "norm_w"]),
        "head_par": np.stack([A[L + "dt_bias"], A[L + "A_log"]], 1),
        "const32": const32,
        "seg_r0": seg_r0.astype(bf),
        "seg_l0": seg_l0.astype(bf),
        "ctx_t": A["ctx_4096"].transpose(0, 2, 1),
        "ctx_n": A["ctx_4096"],
        "w_ffn": A["L0_ffn_weight"].reshape(D, KD, P).transpose(2, 1, 0),
        "gate_w": A["L0_ffn_gate_w"].T,
        "scales": np.tile(np.concatenate([A["L0_ffn_in_channel_scale"], A["L0_ffn_out_channel_scale"]], 1), (3, 1)),
        "lo_rows": lo_rows,
        "ffn_bias": channels(A["L0_ffn_bias"]),
    }
    arrays = {k: np.ascontiguousarray(v) for k, v in arrays.items()}
    nc = bacc.Bacc("TRN2", target_bir_lowering=False, num_devices=1)
    arrays = {f"in_{k}": v for k, v in arrays.items()}
    args = [nc.dram_tensor(k, v.shape, mybir.dt.from_np(v.dtype), kind="ExternalInput").ap() for k, v in arrays.items()]
    out = nc.dram_tensor("out_t", (D, T), F32, kind="ExternalOutput").ap()
    build(nc, *args, out)
    r = run(nc, [arrays], core_ids=[0])
    return np.ascontiguousarray(r.results[0]["out_t"].T).reshape(NB, S, D)
```
